# Optimizing a Trainium2 kernel written in Bass

```python
import numpy as np
import jax
import jax.numpy as jnp

def _softmax(x, axis=-1):
    return jax.nn.softmax(x, axis=axis)
def _gelu(x):
    return jax.nn.gelu(x, approximate=True)
def _silu(x):
    return jax.nn.silu(x)
def _sigmoid(x):
    return jax.nn.sigmoid(x)
def _layernorm(x, axis=-1, eps=1e-5):
    m = jnp.mean(x, axis=axis, keepdims=True)
    v = jnp.var(x, axis=axis, keepdims=True)
    return (x - m) / jnp.sqrt(v + eps)
def _scatter_add(tgt, idx, src, axis=0):
    return tgt.at[idx].add(src)
def _segment_sum(src, seg, n):
    return jax.ops.segment_sum(src, seg, n)

kernel_name = 'mk_conv_seq_d2_conv_nchw96_ee455e'

def setup_inputs(seed: int = 0):
    np.random.seed(seed)
    _w = jnp.asarray
    def _rec_inputs():
        import jax
        import jax.numpy as jnp
        _gk = jax.random.key(seed)
        x = -0.0003483 + 1 * jax.random.normal(jax.random.fold_in(_gk, 1), (16, 96, 96, 96), jnp.float32)
        return x
    x = _rec_inputs()
    def _L0_conv_setup():
        import jax, jax.numpy as jnp
        import numpy as np
        B, C, H, W = (16, 96, 96, 96)
        K, N, R, CR = (4, 8, 6, 12)

        def channel_ln(x, g, b, eps=1e-06):
            mu = jnp.mean(x, axis=1, keepdims=True)
            var = jnp.var(x, axis=1, keepdims=True)
            return (x - mu) * jax.lax.rsqrt(var + eps) * g[None, :, None, None] + b[None, :, None, None]

        def conv1x1(x, w, b):
            return jnp.einsum('bchw,dc->bdhw', x, w) + b[None, :, None, None]

        def ss2d(x, xproj_w, dtproj_w, dtproj_b, A_logs, Ds, g, bta):
            Bq, Cq, Hq, Wq = x.shape
            L = Hq * Wq
            xf = x.reshape(Bq, Cq, L)
            xt = jnp.transpose(x, (0, 1, 3, 2)).reshape(Bq, Cq, L)
            xs = jnp.stack([xf, xt, xf[..., ::-1], xt[..., ::-1]], axis=1)
            x_dbl = jnp.einsum('bkcl,kdc->bkdl', xs, xproj_w)
            dts, Bs, Cs = jnp.split(x_dbl, [R, R + N], axis=2)
            delta = jax.nn.softplus(jnp.einsum('bkrl,kcr->bkcl', dts, dtproj_w) + dtproj_b[None, :, :, None])
            A = -jnp.exp(A_logs)
            u_t = jnp.moveaxis(xs, -1, 0)
            d_t = jnp.moveaxis(delta, -1, 0)
            B_t = jnp.moveaxis(Bs, -1, 0)
            C_t = jnp.moveaxis(Cs, -1, 0)
            h0 = jnp.zeros((Bq, K, Cq, N), x.dtype)

            @jax.checkpoint
            def step(h, inp):
                u, d, Bv, Cv = inp
                dA = jnp.exp(d[..., None] * A)
                h = dA * h + (d * u)[..., None] * Bv[:, :, None, :]
                return (h, jnp.sum(h * Cv[:, :, None, :], axis=-1))
            _, ys = jax.lax.scan(step, h0, (u_t, d_t, B_t, C_t))
            ys = jnp.moveaxis(ys, 0, -1) + Ds[None, :, :, None] * xs

            def untrans(yk):
                return jnp.transpose(yk.reshape(Bq, Cq, Wq, Hq), (0, 1, 3, 2)).reshape(Bq, Cq, L)
            out = ys[:, 0] + untrans(ys[:, 1]) + ys[:, 2, :, ::-1] + untrans(ys[:, 3][..., ::-1])
            return channel_ln(out.reshape(Bq, Cq, Hq, Wq), g, bta)

        def block_forward(x, ln_g, ln_b, p1_w, p1_b, p2in_w, p2in_b, dw_w, dw_b, xproj_w, dtproj_w, dtproj_b, A_logs, Ds, ssln_g, ssln_b, p2n_g, p2n_b, ca_w1, ca_b1, ca_w2, ca_b2, block_idx):
            h = channel_ln(x, ln_g, ln_b)
            a = jax.nn.silu(conv1x1(h, p1_w, p1_b))
            z = conv1x1(h, p2in_w, p2in_b)
            z = jax.lax.conv_general_dilated(z, dw_w, (1, 1), 'SAME', dimension_numbers=('NCHW', 'OIHW', 'NCHW'), feature_group_count=z.shape[1]) + dw_b[None, :, None, None]
            z = jax.nn.silu(z)
            if block_idx % 2 == 0:
                z = jnp.transpose(z, (0, 1, 3, 2))
            else:
                z = z[:, :, ::-1, ::-1]
            z = ss2d(z, xproj_w, dtproj_w, dtproj_b, A_logs, Ds, ssln_g, ssln_b)
            if block_idx % 2 == 0:
                z = jnp.transpose(z, (0, 1, 3, 2))
            else:
                z = z[:, :, ::-1, ::-1]
            z = channel_ln(z, p2n_g, p2n_b)
            y = a * z
            s = jnp.mean(y, axis=(2, 3))
            att = jax.nn.sigmoid(jnp.einsum('cr,br->bc', ca_w2, jax.nn.silu(jnp.einsum('rc,bc->br', ca_w1, s) + ca_b1)) + ca_b2)
            return x + y * att[:, :, None, None]

        def local_mamba(x, params, block_idx):
            b, c, h, w = x.shape
            h2, w2 = (h // 2, w // 2)
            qs = jnp.stack([x[:, :, :h2, :w2], x[:, :, :h2, w2:], x[:, :, h2:, :w2], x[:, :, h2:, w2:]])
            fn = lambda q, *p: block_forward(q, *p, block_idx)
            outs = jax.vmap(fn)(qs, *params)
            top = jnp.concatenate([outs[0], outs[1]], axis=3)
            bot = jnp.concatenate([outs[2], outs[3]], axis=3)
            return jnp.concatenate([top, bot], axis=2)
        key = jax.random.key(seed)
        ks = jax.random.split(key, 12)
        rn = lambda k, shape, s=1.0: jax.random.normal(k, shape, jnp.float32) * s
        return dict(x=rn(ks[0], (B, C, H, W)), ln_g=jnp.ones((4, C)), ln_b=jnp.zeros((4, C)), p1_w=rn(ks[1], (4, C, C), C ** (-0.5)), p1_b=jnp.zeros((4, C)), p2in_w=rn(ks[2], (4, C, C), C ** (-0.5)), p2in_b=jnp.zeros((4, C)), dw_w=rn(ks[3], (4, C, 1, 3, 3), 1.0 / 3.0), dw_b=jnp.zeros((4, C)), xproj_w=rn(ks[4], (4, K, R + 2 * N, C), C ** (-0.5)), dtproj_w=rn(ks[5], (4, K, C, R), R ** (-0.5)), dtproj_b=rn(ks[6], (4, K, C), 0.1), A_logs=jax.random.uniform(ks[7], (4, K, C, N), jnp.float32, 0.0, 1.0), Ds=jnp.ones((4, K, C)), ssln_g=jnp.ones((4, C)), ssln_b=jnp.zeros((4, C)), p2n_g=jnp.ones((4, C)), p2n_b=jnp.zeros((4, C)), ca_w1=rn(ks[8], (4, CR, C), C ** (-0.5)), ca_b1=jnp.zeros((4, CR)), ca_w2=rn(ks[9], (4, C, CR), CR ** (-0.5)), ca_b2=jnp.zeros((4, C)), block_idx=0)
    _L0_conv_all = _L0_conv_setup()
    _L0_conv_in = {k: v for k, v in _L0_conv_all.items() if k in ('ln_g', 'ln_b', 'p1_w', 'p1_b', 'p2in_w', 'p2in_b', 'dw_w', 'dw_b', 'xproj_w', 'dtproj_w', 'dtproj_b', 'A_logs', 'Ds', 'ssln_g', 'ssln_b', 'p2n_g', 'p2n_b', 'ca_w1', 'ca_b1', 'ca_w2', 'ca_b2', )}
    del _L0_conv_all

    def _L1_conv_setup():
        import jax, jax.numpy as jnp
        import numpy as np
        EPS = 1e-05

        def _bn(x, gamma, beta, mean, var):
            inv = jax.lax.rsqrt(var + EPS)
            return (x - mean[None, :, None, None]) * (gamma * inv)[None, :, None, None] + beta[None, :, None, None]

        def _conv(x, w, stride=1, padding=0, groups=1):
            return jax.lax.conv_general_dilated(x, w, window_strides=(stride, stride), padding=[(padding, padding), (padding, padding)], dimension_numbers=('NCHW', 'OIHW', 'NCHW'), feature_group_count=groups)
        key = jax.random.key(seed)
        ks = jax.random.split(key, 8)
        C, E, Cout = (96, 6, 96)
        M = C * E
        x = jax.random.normal(ks[0], (32, C, 56, 56), dtype=jnp.float32)
        w1 = jax.random.normal(ks[1], (M, C, 1, 1), dtype=jnp.float32) * 0.05
        g1 = jnp.ones((M,), jnp.float32)
        b1 = jnp.zeros((M,), jnp.float32)
        m1 = jax.random.normal(ks[2], (M,), jnp.float32) * 0.1
        v1 = jax.random.uniform(ks[3], (M,), jnp.float32, 0.5, 1.5)
        wd = jax.random.normal(ks[4], (M, 1, 3, 3), dtype=jnp.float32) * 0.1
        g2 = jnp.ones((M,), jnp.float32)
        b2 = jnp.zeros((M,), jnp.float32)
        m2 = jax.random.normal(ks[5], (M,), jnp.float32) * 0.1
        v2 = jax.random.uniform(ks[6], (M,), jnp.float32, 0.5, 1.5)
        w3 = jax.random.normal(ks[7], (Cout, M, 1, 1), dtype=jnp.float32) * 0.05
        g3 = jnp.ones((Cout,), jnp.float32)
        b3 = jnp.zeros((Cout,), jnp.float32)
        m3 = jnp.zeros((Cout,), jnp.float32)
        v3 = jnp.ones((Cout,), jnp.float32)
        return {'x': x, 'w1': w1, 'g1': g1, 'b1': b1, 'm1': m1, 'v1': v1, 'wd': wd, 'g2': g2, 'b2': b2, 'm2': m2, 'v2': v2, 'w3': w3, 'g3': g3, 'b3': b3, 'm3': m3, 'v3': v3}
    _L1_conv_all = _L1_conv_setup()
    _L1_conv_in = {k: v for k, v in _L1_conv_all.items() if k in ('w1', 'g1', 'b1', 'm1', 'v1', 'wd', 'g2', 'b2', 'm2', 'v2', 'w3', 'g3', 'b3', 'm3', 'v3', )}
    del _L1_conv_all

    return {
        "x": x,
        "L0_conv_ln_g": _L0_conv_in["ln_g"],
        "L0_conv_ln_b": _L0_conv_in["ln_b"],
        "L0_conv_p1_w": _L0_conv_in["p1_w"],
        "L0_conv_p1_b": _L0_conv_in["p1_b"],
        "L0_conv_p2in_w": _L0_conv_in["p2in_w"],
        "L0_conv_p2in_b": _L0_conv_in["p2in_b"],
        "L0_conv_dw_w": _L0_conv_in["dw_w"],
        "L0_conv_dw_b": _L0_conv_in["dw_b"],
        "L0_conv_xproj_w": _L0_conv_in["xproj_w"],
        "L0_conv_dtproj_w": _L0_conv_in["dtproj_w"],
        "L0_conv_dtproj_b": _L0_conv_in["dtproj_b"],
        "L0_conv_A_logs": _L0_conv_in["A_logs"],
        "L0_conv_Ds": _L0_conv_in["Ds"],
        "L0_conv_ssln_g": _L0_conv_in["ssln_g"],
        "L0_conv_ssln_b": _L0_conv_in["ssln_b"],
        "L0_conv_p2n_g": _L0_conv_in["p2n_g"],
        "L0_conv_p2n_b": _L0_conv_in["p2n_b"],
        "L0_conv_ca_w1": _L0_conv_in["ca_w1"],
        "L0_conv_ca_b1": _L0_conv_in["ca_b1"],
        "L0_conv_ca_w2": _L0_conv_in["ca_w2"],
        "L0_conv_ca_b2": _L0_conv_in["ca_b2"],
        "L1_conv_w1": _L1_conv_in["w1"],
        "L1_conv_g1": _L1_conv_in["g1"],
        "L1_conv_b1": _L1_conv_in["b1"],
        "L1_conv_m1": _L1_conv_in["m1"],
        "L1_conv_v1": _L1_conv_in["v1"],
        "L1_conv_wd": _L1_conv_in["wd"],
        "L1_conv_g2": _L1_conv_in["g2"],
        "L1_conv_b2": _L1_conv_in["b2"],
        "L1_conv_m2": _L1_conv_in["m2"],
        "L1_conv_v2": _L1_conv_in["v2"],
        "L1_conv_w3": _L1_conv_in["w3"],
        "L1_conv_g3": _L1_conv_in["g3"],
        "L1_conv_b3": _L1_conv_in["b3"],
        "L1_conv_m3": _L1_conv_in["m3"],
        "L1_conv_v3": _L1_conv_in["v3"],
    }

def reference(x, L0_conv_ln_g, L0_conv_ln_b, L0_conv_p1_w, L0_conv_p1_b, L0_conv_p2in_w, L0_conv_p2in_b, L0_conv_dw_w, L0_conv_dw_b, L0_conv_xproj_w, L0_conv_dtproj_w, L0_conv_dtproj_b, L0_conv_A_logs, L0_conv_Ds, L0_conv_ssln_g, L0_conv_ssln_b, L0_conv_p2n_g, L0_conv_p2n_b, L0_conv_ca_w1, L0_conv_ca_b1, L0_conv_ca_w2, L0_conv_ca_b2, L1_conv_w1, L1_conv_g1, L1_conv_b1, L1_conv_m1, L1_conv_v1, L1_conv_wd, L1_conv_g2, L1_conv_b2, L1_conv_m2, L1_conv_v2, L1_conv_w3, L1_conv_g3, L1_conv_b3, L1_conv_m3, L1_conv_v3):
    import jax
    import jax.numpy as jnp
    def _L0_conv_ref(x, ln_g, ln_b, p1_w, p1_b, p2in_w, p2in_b, dw_w, dw_b, xproj_w, dtproj_w, dtproj_b, A_logs, Ds, ssln_g, ssln_b, p2n_g, p2n_b, ca_w1, ca_b1, ca_w2, ca_b2, block_idx):
        import jax, jax.numpy as jnp
        import numpy as np
        B, C, H, W = (16, 96, 96, 96)
        K, N, R, CR = (4, 8, 6, 12)

        def channel_ln(x, g, b, eps=1e-06):
            mu = jnp.mean(x, axis=1, keepdims=True)
            var = jnp.var(x, axis=1, keepdims=True)
            return (x - mu) * jax.lax.rsqrt(var + eps) * g[None, :, None, None] + b[None, :, None, None]

        def conv1x1(x, w, b):
            return jnp.einsum('bchw,dc->bdhw', x, w) + b[None, :, None, None]

        def ss2d(x, xproj_w, dtproj_w, dtproj_b, A_logs, Ds, g, bta):
            Bq, Cq, Hq, Wq = x.shape
            L = Hq * Wq
            xf = x.reshape(Bq, Cq, L)
            xt = jnp.transpose(x, (0, 1, 3, 2)).reshape(Bq, Cq, L)
            xs = jnp.stack([xf, xt, xf[..., ::-1], xt[..., ::-1]], axis=1)
            x_dbl = jnp.einsum('bkcl,kdc->bkdl', xs, xproj_w)
            dts, Bs, Cs = jnp.split(x_dbl, [R, R + N], axis=2)
            delta = jax.nn.softplus(jnp.einsum('bkrl,kcr->bkcl', dts, dtproj_w) + dtproj_b[None, :, :, None])
            A = -jnp.exp(A_logs)
            u_t = jnp.moveaxis(xs, -1, 0)
            d_t = jnp.moveaxis(delta, -1, 0)
            B_t = jnp.moveaxis(Bs, -1, 0)
            C_t = jnp.moveaxis(Cs, -1, 0)
            h0 = jnp.zeros((Bq, K, Cq, N), x.dtype)

            @jax.checkpoint
            def step(h, inp):
                u, d, Bv, Cv = inp
                dA = jnp.exp(d[..., None] * A)
                h = dA * h + (d * u)[..., None] * Bv[:, :, None, :]
                return (h, jnp.sum(h * Cv[:, :, None, :], axis=-1))
            _, ys = jax.lax.scan(step, h0, (u_t, d_t, B_t, C_t))
            ys = jnp.moveaxis(ys, 0, -1) + Ds[None, :, :, None] * xs

            def untrans(yk):
                return jnp.transpose(yk.reshape(Bq, Cq, Wq, Hq), (0, 1, 3, 2)).reshape(Bq, Cq, L)
            out = ys[:, 0] + untrans(ys[:, 1]) + ys[:, 2, :, ::-1] + untrans(ys[:, 3][..., ::-1])
            return channel_ln(out.reshape(Bq, Cq, Hq, Wq), g, bta)

        def block_forward(x, ln_g, ln_b, p1_w, p1_b, p2in_w, p2in_b, dw_w, dw_b, xproj_w, dtproj_w, dtproj_b, A_logs, Ds, ssln_g, ssln_b, p2n_g, p2n_b, ca_w1, ca_b1, ca_w2, ca_b2, block_idx):
            h = channel_ln(x, ln_g, ln_b)
            a = jax.nn.silu(conv1x1(h, p1_w, p1_b))
            z = conv1x1(h, p2in_w, p2in_b)
            z = jax.lax.conv_general_dilated(z, dw_w, (1, 1), 'SAME', dimension_numbers=('NCHW', 'OIHW', 'NCHW'), feature_group_count=z.shape[1]) + dw_b[None, :, None, None]
            z = jax.nn.silu(z)
            if block_idx % 2 == 0:
                z = jnp.transpose(z, (0, 1, 3, 2))
            else:
                z = z[:, :, ::-1, ::-1]
            z = ss2d(z, xproj_w, dtproj_w, dtproj_b, A_logs, Ds, ssln_g, ssln_b)
            if block_idx % 2 == 0:
                z = jnp.transpose(z, (0, 1, 3, 2))
            else:
                z = z[:, :, ::-1, ::-1]
            z = channel_ln(z, p2n_g, p2n_b)
            y = a * z
            s = jnp.mean(y, axis=(2, 3))
            att = jax.nn.sigmoid(jnp.einsum('cr,br->bc', ca_w2, jax.nn.silu(jnp.einsum('rc,bc->br', ca_w1, s) + ca_b1)) + ca_b2)
            return x + y * att[:, :, None, None]

        def local_mamba(x, params, block_idx):
            b, c, h, w = x.shape
            h2, w2 = (h // 2, w // 2)
            qs = jnp.stack([x[:, :, :h2, :w2], x[:, :, :h2, w2:], x[:, :, h2:, :w2], x[:, :, h2:, w2:]])
            fn = lambda q, *p: block_forward(q, *p, block_idx)
            outs = jax.vmap(fn)(qs, *params)
            top = jnp.concatenate([outs[0], outs[1]], axis=3)
            bot = jnp.concatenate([outs[2], outs[3]], axis=3)
            return jnp.concatenate([top, bot], axis=2)
        params = (ln_g, ln_b, p1_w, p1_b, p2in_w, p2in_b, dw_w, dw_b, xproj_w, dtproj_w, dtproj_b, A_logs, Ds, ssln_g, ssln_b, p2n_g, p2n_b, ca_w1, ca_b1, ca_w2, ca_b2)
        return local_mamba(x, params, block_idx)

    def _L1_conv_ref(x, w1, g1, b1, m1, v1, wd, g2, b2, m2, v2, w3, g3, b3, m3, v3):
        import jax, jax.numpy as jnp
        import numpy as np
        EPS = 1e-05

        def _bn(x, gamma, beta, mean, var):
            inv = jax.lax.rsqrt(var + EPS)
            return (x - mean[None, :, None, None]) * (gamma * inv)[None, :, None, None] + beta[None, :, None, None]

        def _conv(x, w, stride=1, padding=0, groups=1):
            return jax.lax.conv_general_dilated(x, w, window_strides=(stride, stride), padding=[(padding, padding), (padding, padding)], dimension_numbers=('NCHW', 'OIHW', 'NCHW'), feature_group_count=groups)
        M = wd.shape[0]
        out = jax.nn.relu(_bn(_conv(x, w1), g1, b1, m1, v1))
        out = jax.nn.relu(_bn(_conv(out, wd, stride=1, padding=1, groups=M), g2, b2, m2, v2))
        out = _bn(_conv(out, w3), g3, b3, m3, v3)
        return out + x

    def _gn(v, G=32, eps=1e-5):
        B_, C_, H_, W_ = v.shape
        g = v.reshape(B_, G, C_ // G, H_, W_)
        m = jnp.mean(g, axis=(2, 3, 4), keepdims=True)
        s = jnp.var(g, axis=(2, 3, 4), keepdims=True)
        return ((g - m) / jnp.sqrt(s + eps)).reshape(v.shape)

    def _ln_c(v, eps=1e-6):
        m = jnp.mean(v, axis=1, keepdims=True)
        s = jnp.var(v, axis=1, keepdims=True)
        return (v - m) / jnp.sqrt(s + eps)

    def _ln_t(v, eps=1e-5):
        m = jnp.mean(v, axis=-1, keepdims=True)
        s = jnp.var(v, axis=-1, keepdims=True)
        return (v - m) / jnp.sqrt(s + eps)

    def _to_tokens(v):
        B_, C_, H_, W_ = v.shape
        return v.reshape(B_, C_, H_ * W_).transpose(0, 2, 1)
    def _from_tokens(t, like):
        B_, C_, H_, W_ = like.shape
        return t.transpose(0, 2, 1).reshape(B_, C_, H_, W_)

    x = _L0_conv_ref(x, L0_conv_ln_g, L0_conv_ln_b, L0_conv_p1_w, L0_conv_p1_b, L0_conv_p2in_w, L0_conv_p2in_b, L0_conv_dw_w, L0_conv_dw_b, L0_conv_xproj_w, L0_conv_dtproj_w, L0_conv_dtproj_b, L0_conv_A_logs, L0_conv_Ds, L0_conv_ssln_g, L0_conv_ssln_b, L0_conv_p2n_g, L0_conv_p2n_b, L0_conv_ca_w1, L0_conv_ca_b1, L0_conv_ca_w2, L0_conv_ca_b2, 0)
    x = _L1_conv_ref(x, L1_conv_w1, L1_conv_g1, L1_conv_b1, L1_conv_m1, L1_conv_v1, L1_conv_wd, L1_conv_g2, L1_conv_b2, L1_conv_m2, L1_conv_v2, L1_conv_w3, L1_conv_g3, L1_conv_b3, L1_conv_m3, L1_conv_v3)
    return x


_drawn_inputs = setup_inputs


def setup_inputs(seed=0):
    import zlib

    import numpy as np

    out = dict(_drawn_inputs(seed))
    spreads = {'L0_conv_ln_g': (1.0, 0.2),
     'L0_conv_ln_b': (0.0, 0.1),
     'L0_conv_p1_b': (0.0, 0.27),
     'L0_conv_p2in_b': (0.0, 0.1),
     'L0_conv_dw_b': (0.0, 0.1),
     'L0_conv_Ds': (1.0, 0.2),
     'L0_conv_ssln_g': (1.0, 0.2),
     'L0_conv_ssln_b': (0.0, 0.274),
     'L0_conv_p2n_g': (1.0, 0.2),
     'L0_conv_p2n_b': (0.0, 0.267),
     'L0_conv_ca_b1': (0.0, 0.8),
     'L0_conv_ca_b2': (0.0, 0.524),
     'L1_conv_g1': (1.0, 0.6),
     'L1_conv_b1': (0.0, 0.432),
     'L1_conv_g2': (1.0, 0.2),
     'L1_conv_b2': (0.0, 0.1),
     'L1_conv_g3': (1.0, 0.2),
     'L1_conv_b3': (0.0, 0.1),
     'L1_conv_m3': (0.0, 0.1),
     'L1_conv_v3': (1.0, 0.6)}
    factors = {'L0_conv_dtproj_b': 4.782,
     'L0_conv_ca_w1': 8.0,
     'L0_conv_ca_w2': 7.662,
     'L1_conv_v1': 3.22}
    for name, (base, spread) in spreads.items():
        noise = np.random.default_rng([zlib.crc32(name.encode()), seed]).standard_normal(out[name].shape)
        drawn = base * np.exp(spread * noise) if base else spread * noise
        out[name] = jnp.asarray(drawn.astype(out[name].dtype))
    for name, factor in factors.items():
        out[name] = (out[name] * factor).astype(out[name].dtype)
    return out
```

```python
from contextlib import ExitStack

import numpy as np

import concourse.bass as bass
from concourse import mybir

F32 = mybir.dt.float32
BF16 = mybir.dt.bfloat16
ALU = mybir.AluOpType
ACT = mybir.ActivationFunctionType
ds = bass.ds

C = 96
HQ = 48
L = HQ * HQ
NQ = 4
N = 8
R = 6
CR = 12
IMGS = 4
TILES = IMGS * C // 128
PARTS = 3
NCH = 3
CH = L // NCH
CROWS = HQ // NCH
HALF = CH // 2
BANK = 512
LN_EPS = 1e-6
LN_EXP = "natural_log_exp_and_others"
BN_EPS = 1e-5
ONE = 1


class Memory:

    def __init__(self, nc, ctx, tag):
        self.nc, self.ctx, self.tag = nc, ctx, tag
        self.sems = []

    def sbuf(self, name, shape, dtype=F32):
        return self.ctx.enter_context(self.nc.sbuf_tensor(f"{self.tag}_{name}", shape, dtype))

    def psum(self, name, shape):
        return self.ctx.enter_context(self.nc.psum_tensor(f"{self.tag}_{name}", shape, F32))

    def sem(self, name):
        self.sems.append(self.ctx.enter_context(self.nc.semaphore(f"{self.tag}_{name}")))
        return self.sems[-1]

    def start(self):
        with self.nc.Block() as block:
            @block.sync
            def _(sp):
                for sem in self.sems:
                    sp.sem_inc(sem, ONE)


def halves(ap):
    return ap[:, :, 0:HALF]


def in_halves(ap):
    return ap.rearrange("p (b f) -> p b f", b=2)


def sp_wait(sp, passed, *pairs):
    for sem, value in pairs:
        sp.wait_ge(sem, value)
        sp.sem_inc(passed, 1)


def front_phase(nc, d):
    imgs = d["x"].shape[1]
    TAPS = [(dy, dx) for dy in range(3) for dx in range(3)]
    PE_TAPS = 2
    PAD = HQ + 2

    with ExitStack() as ctx:
        m = Memory(nc, ctx, "front")
        w1all = m.sbuf("w1all", [C, NQ, C])
        w2all = m.sbuf("w2all", [C, NQ, C])
        wxall = m.sbuf("wxall", [C, NQ, 2, 64])
        dwall = m.sbuf("dwall", [C, NQ, 9])
        vec = m.sbuf("vec", [C, NQ, 5])
        center = m.sbuf("center", [C, C])
        mean = m.sbuf("mean", [C, C])
        ident = m.sbuf("ident", [C, C])
        eps = m.sbuf("eps", [C, 1])
        w1raw = m.sbuf("w1raw", [C, C])
        w2raw = m.sbuf("w2raw", [C, C])
        w1 = m.sbuf("w1", [C, C])
        w2 = m.sbuf("w2", [C, C])
        wx = m.sbuf("wx", [C, 2, 64])
        dw = m.sbuf("dw", [C, 9])
        diag = m.sbuf("diag", [C, PE_TAPS, C])
        cur = m.sbuf("cur", [C, 5])
        bias = m.sbuf("bias", [C, 2])
        x = [m.sbuf(f"x{i}", [C, L]) for i in range(2)]
        sq = m.sbuf("sq", [C, CH])
        logv = m.sbuf("logv", [C, CH])
        rstd = m.sbuf("rstd", [C, CH])
        h = m.sbuf("h", [C, CH])
        pad = [m.sbuf(f"pad{i}", [C, PAD, PAD]) for i in range(2)]
        apre = m.sbuf("apre", [C, L])
        a = m.sbuf("a", [C, L])
        zpre = m.sbuf("zpre", [C, L])
        zrow = m.sbuf("zrow", [C, L])
        zcol = m.sbuf("zcol", [C, L])
        proj = m.sbuf("proj", [128, L])
        rest = m.sbuf("rest", [128, CH])
        parts = [m.sbuf(f"part{j}", [128, L], BF16) for j in range(PARTS)]
        ps_x = m.psum("ps_x", [C, 2, BANK])
        ps_w = m.psum("ps_w", [C, 2, BANK])
        ps_d = m.psum("ps_d", [C, 2, BANK])
        ps_p = m.psum("ps_p", [128, 2, BANK])

        w_in = m.sem("w_in")
        passed = m.sem("passed")
        x_in = [m.sem(f"x_in{i}") for i in range(2)]
        a_out = m.sem("a_out")
        zrow_out = m.sem("zrow_out")
        zcol_out = m.sem("zcol_out")
        parts_out = m.sem("parts_out")
        prep_raw = m.sem("prep_raw")
        prep_fold = m.sem("prep_fold")
        prep_bias = m.sem("prep_bias")
        prep_done = m.sem("prep_done")
        pads_zeroed = m.sem("pads_zeroed")
        xc_ready = m.sem("xc_ready")
        sq_ready = m.sem("sq_ready")
        var_ready = m.sem("var_ready")
        log_done = m.sem("log_done")
        rstd_ready = m.sem("rstd_ready")
        h_done = m.sem("h_done")
        conv1_ready = m.sem("conv1_ready")
        conv2_ready = m.sem("conv2_ready")
        apre_done = m.sem("apre_done")
        pad_done = m.sem("pad_done")
        a_done = m.sem("a_done")
        taps_ready = m.sem("taps_ready")
        dve_tap = m.sem("dve_tap")
        zpre_done = m.sem("zpre_done")
        zrow_done = m.sem("zrow_done")
        zcol_done = m.sem("zcol_done")
        proj_ready = m.sem("proj_ready")
        proj_copied = m.sem("proj_copied")
        rest_done = m.sem("rest_done")
        mid_done = m.sem("mid_done")
        parts_done = m.sem("parts_done")

        DVE_TAPS = len(TAPS) - PE_TAPS

        def rows(j):
            return slice(j * CH, (j + 1) * CH)

        def window(buf, j, tap):
            dy, dx = TAPS[tap]
            return buf[:, j * CROWS + dy:(j + 1) * CROWS + dy, dx:dx + HQ].rearrange("p (b r) w -> p b r w", b=2)

        def image(ps):
            return ps[:, :, 0:HALF].rearrange("p b (r w) -> p b r w", w=HQ)

        def run(eng, prepare, slot):
            with eng.Fori(0, NQ) as q:
                base = q * imgs
                prepare(q)
                slot(base, None, None, 0)
                slot(base + 1, base, None, 1)
                with eng.Fori(0, (imgs - 2) // 2) as i:
                    two = base + i * 2
                    slot(two + 2, two + 1, two, 0)
                    slot(two + 3, two + 2, two + 1, 1)
                slot(None, base + (imgs - 1), base + (imgs - 2), 0)
                slot(None, None, base + (imgs - 1), 1)

        nothing = lambda *_: None
        total = NQ * imgs
        m.start()
        nc_block = ctx.enter_context(nc.Block())

        @nc_block.sync
        def _(sp):
            loads = [(w1all, "p1_w"), (w2all, "p2in_w"), (wxall, "xproj_w"), (dwall, "dw_w"), (vec, "front_vec"),
                     (center, "center"), (mean, "mean"), (ident, "ident")]
            for tile, name in loads:
                src = d[name] if name != "ident" else d[name][0:C, 0:C]
                sp.dma_start(tile[tuple([slice(None)] * len(tile.shape))], src).then_inc(w_in, 16)

            def load_x(mi, parity):
                sp.dma_start(x[parity][:, :], d["x_flat"][ds(mi * C, C), :]).then_inc(x_in[parity], 16)

            def slot(mf, mb, mp, parity):
                after = None if mf is None else sp.snap((mf + 1) % total)
                place = None if mp is None else (sp.snap(mp // IMGS), sp.snap(mp % IMGS))
                if mf is not None:
                    sp_wait(sp, passed, (xc_ready, ONE + mf * NCH))
                    load_x(after, 1 - parity)
                end(mf, mb, mp, place)

            def end(mf, mb, mp, place):
                if mf is not None:
                    sp_wait(sp, passed, (a_done, ONE + mf + 1))
                    sp.dma_start(d["a"][ds(mf * C, C), :], a[:, :]).then_inc(a_out, 16)
                if mb is not None:
                    sp_wait(sp, passed, (zrow_done, ONE + mb + 1))
                    sp.dma_start(d["z"][1, ds(mb * C, C), :], zrow[:, :]).then_inc(zrow_out, 16)
                    sp_wait(sp, passed, (zcol_done, ONE + mb + 1))
                    sp.dma_start(d["z"][0, ds(mb * C, C), :], zcol[:, :]).then_inc(zcol_out, 16)
                if mp is not None:
                    sp_wait(sp, passed, (parts_done, ONE + NCH * (mp + 1)), (proj_copied, ONE + 2 * NCH * (mp + 1)))
                    st, im = place
                    for o in range(2):
                        for j in range(PARTS):
                            for k in range(2):
                                for r in range(2):
                                    lo = 64 * o + 16 * k + 8 * r
                                    sp.dma_start(d["bc"][ds(st, 1), o, k, r, ds(im, 1), N * j:N * (j + 1), :]
                                                 .rearrange("s i n l -> (s i n) l"),
                                                 parts[j][lo:lo + N, :]).then_inc(parts_out, 16)
                        for r in range(2):
                            lo = 64 * o + 32 + R * r
                            sp.dma_start(d["dts4"][ds(st, 1), o, r, ds(im, 1), :, :].rearrange("s i k l -> (s i k) l"),
                                         proj[lo:lo + R, :]).then_inc(parts_out, 16)

            load_x(0, 0)
            run(sp, nothing, slot)
            sp_wait(sp, passed, (x_in[0], ONE + 16 * (total // 2 + 1)))
            for sem, n in ((a_out, total), (zrow_out, total), (zcol_out, total), (parts_out, total * 28)):
                sp_wait(sp, passed, (sem, ONE + 16 * n))

        @nc_block.tensor
        def _(pe):
            def prepare(q):
                pe.wait_ge(prep_raw, ONE + q + 1)
                pe.matmul(ps_w[:, 0, 0:1], w1raw[:, :], cur[:, 1:2], start=True, stop=True)
                pe.matmul(ps_w[:, 1, 0:1], w2raw[:, :], cur[:, 1:2], start=True, stop=True).then_inc(prep_bias, 1)
                pe.wait_ge(prep_done, ONE + q + 1)

            def front(mi, j, parity):
                k = mi * NCH + j
                pe.wait_ge(x_in[parity], ONE + 16 * (mi // 2 + 1))
                pe.wait_ge(h_done, ONE + k)
                for b in range(2):
                    mm = pe.matmul(ps_x[:, b, 0:HALF], center[:, :], x[parity][:, j * CH + b * HALF:j * CH + (b + 1) * HALF], start=True, stop=True)
                mm.then_inc(xc_ready, 1)

            def front2(mi, j, parity):
                k = mi * NCH + j
                pe.wait_ge(sq_ready, ONE + k + 1)
                pe.wait_ge(pad_done, ONE + k)
                for b in range(2):
                    mm = pe.matmul(ps_w[:, b, 0:HALF], mean[:, :], sq[:, b * HALF:(b + 1) * HALF], start=True, stop=True)
                mm.then_inc(var_ready, 1)

            def front3(mi, j, parity):
                k = mi * NCH + j
                pe.wait_ge(h_done, ONE + k + 1)
                for b in range(2):
                    mm = pe.matmul(ps_w[:, b, 0:HALF], w1[:, :], h[:, b * HALF:(b + 1) * HALF], start=True, stop=True)
                mm.then_inc(conv1_ready, 1)
                pe.wait_ge(apre_done, ONE + k + 1)
                for b in range(2):
                    mm = pe.matmul(ps_w[:, b, 0:HALF], w2[:, :], h[:, b * HALF:(b + 1) * HALF], start=True, stop=True)
                mm.then_inc(conv2_ready, 1)

            def back(mi, j, parity):
                k = mi * NCH + j
                pe.wait_ge(pad_done, ONE + NCH * (mi + 1))
                pe.wait_ge(zpre_done, ONE + k)
                for tap in range(PE_TAPS):
                    for b in range(2):
                        mm = pe.matmul(image(ps_d)[:, b], diag[:, tap, :], window(pad[parity], j, tap)[:, b],
                                       start=(tap == 0), stop=(tap == PE_TAPS - 1))
                mm.then_inc(taps_ready, 1)

            def project(mi, j):
                k = mi * NCH + j
                pe.wait_ge(zrow_done, ONE + mi + 1)
                pe.wait_ge(zcol_done, ONE + mi + 1)
                pe.wait_ge(proj_copied, ONE + 2 * k)
                pe.wait_ge(rest_done, ONE + k)
                for o, src in enumerate((zcol, zrow)):
                    for b in range(2):
                        lo = j * CH + b * HALF
                        mm = pe.matmul(ps_p[64 * o:64 * (o + 1), b, 0:HALF], wx[:, o, :], src[:, lo:lo + HALF], start=True, stop=True)
                mm.then_inc(proj_ready, 1)

            def slot(mf, mb, mp, parity):
                for j in range(NCH):
                    if mf is not None:
                        front(mf, j, parity)
                    if mb is not None:
                        back(mb, j, 1 - parity)
                    if mf is not None:
                        front2(mf, j, parity)
                    if mp is not None:
                        project(mp, j)
                    if mf is not None:
                        front3(mf, j, parity)

            run(pe, prepare, slot)

        @nc_block.scalar
        def _(act):
            def prepare(q):
                act.wait_ge(prep_done, ONE + q + 1)

            def front(mi, j, parity):
                k = mi * NCH + j
                act.wait_ge(xc_ready, ONE + k + 1)
                act.wait_ge(var_ready, ONE + k)
                act.activation(sq[:, :].rearrange("p (b f) -> p b f", b=2), halves(ps_x), ACT.Square).then_inc(sq_ready, 1)
                act.wait_ge(var_ready, ONE + k + 1)
                act.activation(logv[:, :].rearrange("p (b f) -> p b f", b=2), halves(ps_w), ACT.Ln, bias=eps[:, 0:1]).then_inc(log_done, 1)
                act.wait_ge(log_done, ONE + k + 1)
                act.wait_ge(h_done, ONE + k)
                act.activation(rstd[:, :], logv[:, :], ACT.Exp, scale=-0.5).then_inc(rstd_ready, 1)

            def front2(mi, j, parity):
                k = mi * NCH + j
                act.wait_ge(conv1_ready, ONE + k + 1)
                if j == 0:
                    act.wait_ge(a_done, ONE + mi)
                act.activation(apre[:, rows(j)].rearrange("p (b f) -> p b f", b=2), halves(ps_w), ACT.Identity,
                               bias=bias[:, 0:1]).then_inc(apre_done, 1)
                act.wait_ge(conv2_ready, ONE + k + 1)
                out = pad[parity][:, 1 + j * CROWS:1 + (j + 1) * CROWS, 1:1 + HQ].rearrange("p (b r) w -> p b r w", b=2)
                act.activation(out, image(ps_w), ACT.Identity, bias=bias[:, 1:2]).then_inc(pad_done, 1)

            def project(mi, j):
                k = mi * NCH + j
                act.wait_ge(proj_ready, ONE + k + 1)
                act.wait_ge(parts_out, ONE + 16 * 28 * mi)
                for dst in (proj, parts[0]):
                    act.activation(dst[:, rows(j)].rearrange("p (b f) -> p b f", b=2), halves(ps_p), ACT.Copy).then_inc(proj_copied, 1)

            def end(mf, mb, mp):
                if mf is not None:
                    act.wait_ge(apre_done, ONE + NCH * (mf + 1))
                    act.wait_ge(a_out, ONE + 16 * mf)
                    act.activation(a[:, :], apre[:, :], ACT.Silu).then_inc(a_done, 1)
                if mb is not None:
                    act.wait_ge(zpre_done, ONE + NCH * (mb + 1))
                    act.wait_ge(zrow_out, ONE + 16 * mb)
                    act.wait_ge(proj_ready, ONE + NCH * mb)
                    act.activation(zrow[:, :], zpre[:, :], ACT.Silu, bias=cur[:, 4:5]).then_inc(zrow_done, 1)

            def slot(mf, mb, mp, parity):
                for j in range(NCH):
                    if mf is not None:
                        front(mf, j, parity)
                    if mp is not None:
                        project(mp, j)
                    if mf is not None:
                        front2(mf, j, parity)
                end(mf, mb, mp)
                act.preload_act_table_set(LN_EXP)

            act.preload_act_table_set(LN_EXP)
            act.wait_ge(pads_zeroed, ONE + 3)
            run(act, prepare, slot)

        @nc_block.vector
        def _(dve):
            def prepare(q):
                dve.wait_ge(proj_ready, ONE + q * (imgs * NCH))
                dve.wait_ge(zrow_done, ONE + q * imgs)
                dve.tensor_copy(cur[:, :], vec[:, ds(q, 1), :].rearrange("p a v -> p (a v)"))
                dve.tensor_copy(w1raw[:, :], w1all[:, ds(q, 1), :].rearrange("p a v -> p (a v)"))
                dve.tensor_copy(w2raw[:, :], w2all[:, ds(q, 1), :].rearrange("p a v -> p (a v)"))
                dve.tensor_copy(wx[:, :, :], wxall[:, ds(q, 1), :, :].rearrange("p a o v -> p (a o) v"))
                dve.tensor_copy(dw[:, :], dwall[:, ds(q, 1), :].rearrange("p a v -> p (a v)")).then_inc(prep_raw, 1)
                dve.wait_ge(prep_raw, ONE + q + 1)
                dve.tensor_scalar(w1[:, :], w1raw[:, :], cur[:, 0:1], None, ALU.mult)
                dve.tensor_scalar(w2[:, :], w2raw[:, :], cur[:, 0:1], None, ALU.mult)
                for tap in range(PE_TAPS):
                    dve.tensor_scalar(diag[:, tap, :], ident[:, :], dw[:, tap:tap + 1], None, ALU.mult)
                dve.wait_ge(prep_bias, ONE + q + 1)
                dve.tensor_tensor(bias[:, 0:1], ps_w[:, 0, 0:1], cur[:, 2:3], ALU.add)
                dve.tensor_tensor(bias[:, 1:2], ps_w[:, 1, 0:1], cur[:, 3:4], ALU.add).then_inc(prep_done, 1)
                dve.wait_ge(prep_done, ONE + q + 1)

            def front(mi, j, parity):
                k = mi * NCH + j
                dve.wait_ge(rstd_ready, ONE + k + 1)
                dve.wait_ge(conv2_ready, ONE + k)
                dve.tensor_tensor(h[:, :].rearrange("p (b f) -> p b f", b=2), halves(ps_x),
                                  rstd[:, :].rearrange("p (b f) -> p b f", b=2), ALU.mult).then_inc(h_done, 1)

            def back(mi, j, parity, taps):
                k = mi * NCH + j
                for t in taps:
                    tap = PE_TAPS + t
                    if t == 0:
                        dve.wait_ge(taps_ready, ONE + k + 1)
                    else:
                        dve.wait_ge(dve_tap, ONE + k * (DVE_TAPS - 1) + t)
                    last = t == DVE_TAPS - 1
                    if last:
                        if j == 0:
                            dve.wait_ge(zrow_done, ONE + mi)
                        out = zpre[:, rows(j)].rearrange("p (b r w) -> p b r w", b=2, w=HQ)
                    else:
                        out = image(ps_d)
                    ins = dve.scalar_tensor_tensor(out=out, in0=window(pad[parity], j, tap), scalar=dw[:, tap:tap + 1],
                                                   in1=image(ps_d), op0=ALU.mult, op1=ALU.add)
                    ins.then_inc(zpre_done if last else dve_tap, 1)

            def project(mi, j):
                k = mi * NCH + j
                dve.wait_ge(proj_copied, ONE + 2 * (k + 1))
                dve.wait_ge(parts_done, ONE + k)
                dve.wait_ge(parts_out, ONE + 16 * 28 * mi)
                dve.tensor_tensor(rest[:, :].rearrange("p (b f) -> p b f", b=2), halves(ps_p),
                                  parts[0][:, rows(j)].rearrange("p (b f) -> p b f", b=2), ALU.subtract).then_inc(rest_done, 1)
                dve.wait_ge(rest_done, ONE + k + 1)
                dve.tensor_copy(parts[1][:, rows(j)], rest[:, :]).then_inc(mid_done, 1)

            def slot(mf, mb, mp, parity):
                for j in range(NCH):
                    if mb is not None:
                        back(mb, j, 1 - parity, range(0, 3))
                    if mf is not None:
                        front(mf, j, parity)
                    if mp is not None:
                        project(mp, j)
                    if mb is not None:
                        back(mb, j, 1 - parity, range(3, DVE_TAPS))
                if mb is not None:
                    dve.wait_ge(zrow_done, ONE + mb + 1)
                    dve.wait_ge(zcol_out, ONE + 16 * mb)
                    dve.tensor_copy(zcol[:, :].rearrange("p (w h) -> p w h", w=HQ),
                                    zrow[:, :].rearrange("p (h w) -> p w h", w=HQ)).then_inc(zcol_done, 1)

            for i in range(2):
                dve.memset(pad[i][:, :, :], 0.0).then_inc(pads_zeroed, 1)
            dve.memset(eps[:, :], LN_EPS).then_inc(pads_zeroed, 1)
            dve.wait_ge(w_in, ONE + 16 * 8)
            run(dve, prepare, slot)

        @nc_block.gpsimd
        def _(pool):
            def project(mi, j):
                k = mi * NCH + j
                pool.wait_ge(mid_done, ONE + k + 1)
                pool.tensor_tensor(parts[2][:, rows(j)], rest[:, :], parts[1][:, rows(j)], ALU.subtract).then_inc(parts_done, 1)

            def slot(mf, mb, mp, parity):
                if mp is not None:
                    pool.wait_ge(parts_out, ONE + 16 * 28 * mp)
                    for j in range(NCH):
                        project(mp, j)

            run(pool, nothing, slot)

def scan_phase(nc, d):
    U = d["z"].shape[1] // 128
    UNITS = 4 * NCH * N
    SEG = NCH * N
    SLOTS = 4 * NCH * (N + 1)
    CREDIT = 8
    LAG = 4
    RA, RC, RH = 4, 4, 6

    with ExitStack() as ctx:
        m = Memory(nc, ctx, "scan")
        z = [m.sbuf(f"z{o}", [128, L]) for o in range(2)]
        y = [m.sbuf(f"y{o}", [128, L]) for o in range(2)]
        delta = [m.sbuf(f"delta{r}", [128, L]) for r in range(2)]
        du = [m.sbuf(f"du{r}", [128, L]) for r in range(2)]
        bparts = [m.sbuf(f"bparts{r}", [96, L], BF16) for r in range(2)]
        cparts = [m.sbuf(f"cparts{r}", [96, L], BF16) for r in range(2)]
        dts = [m.sbuf(f"dts{r}", [IMGS * R, L]) for r in range(2)]
        select = [m.sbuf(f"select{o}", [96, N, 128], BF16) for o in range(2)]
        wdt = [m.sbuf(f"wdt{o}", [IMGS * R, 2, 128]) for o in range(2)]
        prm = [m.sbuf(f"prm{o}", [128, 2 * N + 4]) for o in range(2)]
        negA = [m.sbuf(f"negA{o}", [128, 2 * N]) for o in range(2)]
        dsum = [m.sbuf(f"dsum{o}", [128, 1]) for o in range(2)]
        ident = m.sbuf("ident", [128, 128])
        dA = m.sbuf("dA", [128, RA, CH])
        csb = m.sbuf("csb", [128, RC, CH])
        hc = m.sbuf("hc", [128, RH, CH])
        h = m.sbuf("h", [128, N, CH])
        relu = m.sbuf("relu", [128, CH])
        soft = m.sbuf("soft", [128, CH])
        tiny = m.sbuf("tiny", [128, 4])
        ps_b = m.psum("ps_b", [128, 2, 2 * BANK])
        ps_c = m.psum("ps_c", [128, 2 * BANK])
        ps_y = m.psum("ps_y", [128, 2 * BANK])

        const_in = m.sem("const_in")
        passed = m.sem("passed")
        z_in = [m.sem(f"z_in{o}") for o in range(2)]
        prm_in = [m.sem(f"prm_in{o}") for o in range(2)]
        dts_in = [m.sem(f"dts_in{r}") for r in range(2)]
        bc_in = [m.sem(f"bc_in{r}") for r in range(2)]
        y_out = [m.sem(f"y_out{o}") for o in range(2)]
        negA_step = m.sem("negA_step")
        negA_ready = m.sem("negA_ready")
        dsum_ready = m.sem("dsum_ready")
        b_ready = m.sem("b_ready")
        c_ready = m.sem("c_ready")
        c_evac = m.sem("c_evac")
        dA_ready = m.sem("dA_ready")
        dbu_ready = m.sem("dbu_ready")
        scan_done = m.sem("scan_done")
        hc_done = m.sem("hc_done")
        y_summed = m.sem("y_summed")
        y_evac = m.sem("y_evac")
        abs_done = m.sem("abs_done")
        exp_done = m.sem("exp_done")
        soft_ready = m.sem("soft_ready")
        delta_done = m.sem("delta_done")
        du_done = m.sem("du_done")

        order = [list(range(NCH)), list(range(NCH))[::-1]]

        def cols(i, r):
            c = order[r][i]
            return slice(c * CH, (c + 1) * CH)

        def slot(u, s, i, pos):
            return u * SLOTS + (NCH + (s * NCH + i) * (N + 1) + pos)

        def unit(u, s, i, n):
            return u * UNITS + (s * SEG + i * N + n)

        def pos(n):
            return n if n < 2 else n + 1

        def pieces():
            return [(0, BANK), (BANK, CH)]

        def ring(depth, s, i, n):
            return (s * SEG + i * N + n) % depth

        steps = [(s, i, n) for s in range(4) for i in range(NCH) for n in range(N)]

        m.start()
        nc_block = ctx.enter_context(nc.Block())

        @nc_block.sync
        def _(sp):
            def load_z(o, u, t):
                sp.dma_start(z[o][:, :], d["z"][o, ds(u * 128, 128), :]).then_inc(z_in[o], 16)
                sp.dma_start(prm[o][:, :], d["prm"][ds(u, 1), o, :, :].rearrange("a p c -> (a p) c")).then_inc(prm_in[o], 16)
                sp.dma_start(wdt[o][:, :, :], d["wdt"][ds(u, 1), o, :, :, :].rearrange("a k r p -> (a k) r p")).then_inc(prm_in[o], 16)
                sp.dma_start(select[o][:, :, :], d["select"][ds(t, 1), :, :, :].rearrange("a k n p -> (a k) n p")).then_inc(prm_in[o], 16)

            def load_dts(o, r, st):
                sp.dma_start(dts[r][:, :], d["dts"][ds(st, 1), o, r, :, :].rearrange("a k l -> (a k) l")).then_inc(dts_in[r], 16)

            def load_bc(o, r, st):
                for k, t in enumerate((bparts[r], cparts[r])):
                    sp.dma_start(t[:, :], d["bc"][ds(st, 1), o, k, r, :, :, :].rearrange("a i j l -> (a i j) l")).then_inc(bc_in[r], 16)

            sp.dma_start(ident[:, :], d["ident"][:, :]).then_inc(const_in, 16)
            load_dts(0, 0, 0)
            load_z(0, 0, 0)
            load_bc(0, 0, 0)
            load_dts(0, 1, 0)
            with sp.Fori(0, U) as u:
                nxt = sp.snap((u + 1) % U)
                tile, next_tile = sp.snap(u % TILES), sp.snap(nxt % TILES)
                group, next_group = sp.snap(u // TILES), sp.snap(nxt // TILES)
                for s in range(4):
                    o, r = divmod(s, 2)
                    sp_wait(sp, passed, (b_ready, ONE + unit(u, s, 0, 0)), (c_ready, ONE + slot(u, s, 0, 0)))
                    if s == 2:
                        sp_wait(sp, passed, (y_evac, ONE + CREDIT + u * 4 * NCH + 2 * NCH))
                        sp.dma_start(d["y"][0, ds(u * 128, 128), :], y[0][:, :]).then_inc(y_out[0], 16)
                    if s == 0:
                        load_z(1, u, tile)
                    if s == 2:
                        load_z(0, nxt, next_tile)
                    load_dts((o + 1) % 2, r, group if s < 2 else next_group)
                    so, sr = divmod((s + 1) % 4, 2)
                    load_bc(so, sr, group if s < 3 else next_group)
                sp_wait(sp, passed, (y_evac, ONE + CREDIT + u * 4 * NCH + 4 * NCH))
                sp.dma_start(d["y"][1, ds(u * 128, 128), :], y[1][:, :]).then_inc(y_out[1], 16)
            for o in range(2):
                sp_wait(sp, passed, (y_out[o], ONE + 16 * U))
            sp_wait(sp, passed, (z_in[0], ONE + 16 * (U + 1)), (z_in[1], ONE + 16 * U), (prm_in[0], ONE + 48 * (U + 1)), (prm_in[1], ONE + 48 * U))
            for r in range(2):
                sp_wait(sp, passed, (dts_in[r], ONE + 16 * (2 * U + 1)))
            sp_wait(sp, passed, (bc_in[0], ONE + 32 * (2 * U + 1)), (bc_in[1], ONE + 32 * 2 * U))

        @nc_block.tensor
        def _(pe):
            def delta_product(u, s, i, use):
                o, r = divmod(s, 2)
                pe.wait_ge(dts_in[r], ONE + 16 * (2 * u + o + 1))
                pe.wait_ge(prm_in[o], ONE + 48 * (u + 1))
                pe.wait_ge(c_evac, ONE + use)
                a = cols(i, r).start
                for lo, hi in pieces():
                    mm = pe.matmul(ps_c[:, lo:hi], wdt[o][:, r, :], dts[r][:, a + lo:a + hi], start=True, stop=True)
                mm.then_inc(c_ready, 1)

            def spread(u, s, i, n):
                o, r = divmod(s, 2)
                a = cols(i, r).start
                if i == 0 and n == 0:
                    pe.wait_ge(bc_in[r], ONE + 32 * (2 * u + o + 1))
                k = unit(u, s, i, n)
                pe.wait_ge(scan_done, ONE + CREDIT + k - 1)
                for lo, hi in pieces():
                    mm = pe.matmul(ps_b[:, n % 2, lo:hi], select[o][:, n, :], bparts[r][:, a + lo:a + hi], start=True, stop=True)
                mm.then_inc(b_ready, 1)
                pe.wait_ge(c_evac, ONE + slot(u, s, i, pos(n)))
                for lo, hi in pieces():
                    mm = pe.matmul(ps_c[:, lo:hi], select[o][:, n, :], cparts[r][:, a + lo:a + hi], start=True, stop=True)
                mm.then_inc(c_ready, 1)

            def sum_states(u, s, i, n):
                if n == 0:
                    pe.wait_ge(y_evac, ONE + CREDIT + u * 4 * NCH + s * NCH + i)
                pe.wait_ge(hc_done, ONE + CREDIT + unit(u, s, i, n) + 1)
                for lo, hi in pieces():
                    mm = pe.matmul(ps_y[:, lo:hi], ident[:, :], hc[:, ring(RH, s, i, n), lo:hi], start=(n == 0), stop=(n == N - 1))
                mm.then_inc(y_summed, 1)

            pe.wait_ge(const_in, ONE + 16)
            for i in range(NCH):
                delta_product(0, 0, i, i)

            with pe.Fori(0, U) as u:
                for k, (s, i, n) in enumerate(steps):
                    spread(u, s, i, n)
                    if n == 1:
                        ns, nu = ((s + 1) % 4, u if s < 3 else u + 1)
                        delta_product(nu, ns, i, slot(u, s, i, 2))
                    if k >= LAG:
                        sum_states(u, *steps[k - LAG])
                for st in steps[-LAG:]:
                    sum_states(u, *st)

        @nc_block.scalar
        def _(act):
            def neg_a(u, o):
                act.wait_ge(prm_in[o], ONE + 48 * (u + 1))
                act.activation(negA[o][:, :], prm[o][:, 0:2 * N], ACT.Exp).then_inc(negA_step, 1)
                act.wait_ge(negA_step, ONE + 2 * u + (o + 1))
                act.activation(negA[o][:, :], negA[o][:, :], ACT.Copy, scale=-1.0).then_inc(negA_ready, 1)

            def softplus_terms(u, s, i, use):
                o, r = divmod(s, 2)
                j = u * 4 * NCH + (s * NCH + i)
                bias = prm[o][:, 2 * N + 2 + r:2 * N + 3 + r]
                act.wait_ge(c_ready, ONE + use + 1)
                act.wait_ge(delta_done, ONE + j)
                act.activation(relu[:, :], ps_c[:, 0:CH], ACT.Relu, bias=bias)
                act.activation(soft[:, :], ps_c[:, 0:CH], ACT.Abs, bias=bias).then_inc(c_evac, 1)

            def softplus_exp(u, s, i, use):
                act.wait_ge(c_evac, ONE + use + 1)
                act.activation(soft[:, :], soft[:, :], ACT.Exp, scale=-1.0).then_inc(exp_done, 1)

            def softplus_log(u, s, i):
                j = u * 4 * NCH + (s * NCH + i)
                act.wait_ge(exp_done, ONE + j + 1)
                act.activation(soft[:, :], soft[:, :], ACT.Ln, bias=1.0).then_inc(soft_ready, 1)

            def decay(u, s, i, n):
                o, r = divmod(s, 2)
                k = unit(u, s, i, n)
                if n == 0:
                    act.wait_ge(delta_done, ONE + u * 4 * NCH + (s * NCH + i) + 1)
                    if i == 0 and r == 0:
                        act.wait_ge(negA_ready, ONE + 2 * u + (o + 1))
                act.wait_ge(scan_done, ONE + CREDIT + k - (RA - 1))
                act.activation(dA[:, ring(RA, s, i, n), :], delta[r][:, cols(i, r)], ACT.Exp,
                               scale=negA[o][:, r * N + n:r * N + n + 1]).then_inc(dA_ready, 1)

            act.preload_act_table_set(LN_EXP)
            neg_a(0, 0)
            for i in range(NCH):
                softplus_terms(0, 0, i, i)
                softplus_exp(0, 0, i, i)
                softplus_log(0, 0, i)
            decay(0, 0, 0, 0)
            with act.Fori(0, U) as u:
                for q, (s, i, n) in enumerate(steps):
                    k = unit(u, s, i, n)
                    if q + 1 < UNITS:
                        decay(u, *steps[q + 1])
                    else:
                        decay(u + 1, *steps[0])
                    act.wait_ge(c_ready, ONE + slot(u, s, i, pos(n)) + 1)
                    act.wait_ge(hc_done, ONE + CREDIT + k - (RC - 1))
                    act.activation(csb[:, ring(RC, s, i, n), :], ps_c[:, 0:CH], ACT.Copy).then_inc(c_evac, 1)
                    ns, nu = ((s + 1) % 4, u if s < 3 else u + 1)
                    if n == 1:
                        softplus_terms(nu, ns, i, slot(u, s, i, 2))
                    if n == 2:
                        softplus_exp(nu, ns, i, slot(u, s, i, 2))
                    if n == 3:
                        softplus_log(nu, ns, i)
                    if (i, n) == (1, 6) and s == 0:
                        neg_a(u, 1)
                    if (i, n) == (1, 6) and s == 2:
                        neg_a(u + 1, 0)

        @nc_block.vector
        def _(dve):
            def add_d(u, o):
                dve.wait_ge(prm_in[o], ONE + 48 * (u + 1))
                dve.tensor_tensor(dsum[o][:, :], prm[o][:, 2 * N:2 * N + 1], prm[o][:, 2 * N + 1:2 * N + 2],
                                  ALU.add).then_inc(dsum_ready, 1)

            def evacuate(u, s, i):
                o, r = divmod(s, 2)
                j = u * 4 * NCH + (s * NCH + i)
                dve.wait_ge(y_summed, ONE + CREDIT + unit(u, s, i, N - 1) + 1)
                part = y[o][:, cols(i, r)]
                if r == 0:
                    dve.wait_ge(dsum_ready, ONE + 2 * u + (o + 1))
                    dve.wait_ge(y_out[o], ONE + 16 * u)
                    dve.scalar_tensor_tensor(out=part, in0=z[o][:, cols(i, r)], scalar=dsum[o][:, 0:1],
                                             in1=ps_y[:, 0:CH], op0=ALU.mult, op1=ALU.add).then_inc(y_evac, 1)
                else:
                    dve.tensor_tensor(part, part, ps_y[:, 0:CH], ALU.add).then_inc(y_evac, 1)

            dve.memset(tiny[:, 0:1], 0.0).then_inc(scan_done, CREDIT)
            dve.memset(tiny[:, 1:2], 0.0).then_inc(y_evac, CREDIT)
            dve.memset(tiny[:, 3:4], 0.0).then_inc(y_summed, CREDIT)
            add_d(0, 0)

            with dve.Fori(0, U) as u:
                for s, i, n in steps:
                    o, r = divmod(s, 2)
                    k = unit(u, s, i, n)
                    j = u * 4 * NCH + (s * NCH + i)
                    if n == 0:
                        dve.wait_ge(du_done, ONE + j + 1)
                    dve.wait_ge(b_ready, ONE + k + 1)
                    dbu = ps_b[:, n % 2, 0:CH]
                    dve.tensor_tensor(dbu, du[r][:, cols(i, r)], dbu, ALU.mult).then_inc(dbu_ready, 1)
                    if n == LAG - 1 and (s, i) != (0, 0):
                        evacuate(u, *divmod(s * NCH + i - 1, NCH))
                    dve.wait_ge(dbu_ready, ONE + k + 1)
                    dve.wait_ge(dA_ready, ONE + k + 1)
                    dve.wait_ge(hc_done, ONE + CREDIT + k - 7)
                    dec, out = dA[:, ring(RA, s, i, n), :], h[:, n, :]
                    if r == 0:
                        first = h[:, n, CH - 1:CH]
                    else:
                        dec, out, dbu = dec[:, ::-1], out[:, ::-1], dbu[:, ::-1]
                        first = h[:, n, 0:1]
                    dve.tensor_tensor_scan(out, dec, dbu, 0.0 if i == 0 else first, ALU.mult, ALU.add).then_inc(scan_done, 1)
                    if (i, n) == (NCH - 1, N - 1):
                        if s == 0:
                            add_d(u, 1)
                        if s == 2:
                            add_d(u + 1, 0)
                evacuate(u, 3, NCH - 1)

        @nc_block.gpsimd
        def _(pool):
            def finish_delta(u, s, i):
                o, r = divmod(s, 2)
                j = u * 4 * NCH + (s * NCH + i)
                pool.wait_ge(soft_ready, ONE + j + 1)
                part = delta[r][:, cols(i, r)]
                pool.tensor_tensor(part, relu[:, :], soft[:, :], ALU.add).then_inc(delta_done, 1)

            def scale_input(u, s, i):
                o, r = divmod(s, 2)
                j = u * 4 * NCH + (s * NCH + i)
                part = delta[r][:, cols(i, r)]
                pool.wait_ge(delta_done, ONE + j + 1)
                pool.wait_ge(z_in[o], ONE + 16 * (u + 1))
                pool.tensor_tensor(du[r][:, cols(i, r)], part, z[o][:, cols(i, r)], ALU.mult).then_inc(du_done, 1)

            pool.memset(tiny[:, 2:3], 0.0).then_inc(hc_done, CREDIT)
            for i in range(NCH):
                finish_delta(0, 0, i)
                scale_input(0, 0, i)
            with pool.Fori(0, U) as u:
                for s, i, n in steps:
                    k = unit(u, s, i, n)
                    pool.wait_ge(c_evac, ONE + slot(u, s, i, pos(n)) + 1)
                    pool.wait_ge(scan_done, ONE + CREDIT + k + 1)
                    pool.wait_ge(y_summed, ONE + CREDIT + k - (RH - 1))
                    pool.tensor_tensor(hc[:, ring(RH, s, i, n), :], h[:, n, :], csb[:, ring(RC, s, i, n), :],
                                       ALU.mult).then_inc(hc_done, 1)
                    ns, nu = ((s + 1) % 4, u if s < 3 else u + 1)
                    if n == 4:
                        finish_delta(nu, ns, i)
                    if n == 6:
                        scale_input(nu, ns, i)

def gate_phase(nc, d):
    imgs = d["x"].shape[1]
    with ExitStack() as ctx:
        m = Memory(nc, ctx, "gate")
        center = m.sbuf("center", [C, C])
        mean = m.sbuf("mean", [C, C])
        eps = m.sbuf("eps", [C, 1])
        vec = m.sbuf("vec", [C, NQ, 5])
        ca1 = m.sbuf("ca1", [C, NQ, CR])
        ca2 = m.sbuf("ca2", [CR, NQ, C])
        cab1 = m.sbuf("cab1", [CR, NQ])
        cur = m.sbuf("cur", [C, 5])
        cg = m.sbuf("cg", [C, C])
        cb = m.sbuf("cb", [C, 1])
        wa1 = m.sbuf("wa1", [C, CR])
        wa2 = m.sbuf("wa2", [CR, C])
        ba1 = m.sbuf("ba1", [CR, 1])
        ycol = [m.sbuf(f"ycol{i}", [C, L]) for i in range(2)]
        yrow = [m.sbuf(f"yrow{i}", [C, L]) for i in range(2)]
        a = [m.sbuf(f"a{i}", [C, L]) for i in range(2)]
        x = [m.sbuf(f"x{i}", [C, L]) for i in range(2)]
        y = [m.sbuf(f"y{i}", [C, L]) for i in range(2)]
        ysum = m.sbuf("ysum", [C, 2, CH])
        sq = m.sbuf("sq", [C, CH])
        sq2 = m.sbuf("sq2", [C, CH])
        logv = m.sbuf("logv", [C, CH])
        logv2 = m.sbuf("logv2", [C, CH])
        rstd = m.sbuf("rstd", [C, CH])
        rstd2 = m.sbuf("rstd2", [C, CH])
        s1 = m.sbuf("s1", [C, CH])
        z2 = m.sbuf("z2", [C, CH])
        z3 = m.sbuf("z3", [C, CH])
        total = [m.sbuf(f"total{i}", [C, NCH]) for i in range(2)]
        hid = m.sbuf("hid", [CR, 5])
        att = m.sbuf("att", [C, 4])
        ps_x = m.psum("ps_x", [C, 2, BANK])
        ps_x2 = m.psum("ps_x2", [C, 2, BANK])
        ps_v = m.psum("ps_v", [C, 2, BANK])
        ps_t = m.psum("ps_t", [C, BANK])

        w_in = m.sem("w_in")
        passed = m.sem("passed")
        y_in = [m.sem(f"y_in{i}") for i in range(2)]
        a_in = [m.sem(f"a_in{i}") for i in range(2)]
        x_in = [m.sem(f"x_in{i}") for i in range(2)]
        x_out = [m.sem(f"x_out{i}") for i in range(2)]
        eps_set = m.sem("eps_set")
        prep_raw = m.sem("prep_raw")
        prep_cb = m.sem("prep_cb")
        prep_done = m.sem("prep_done")
        ysum_done = m.sem("ysum_done")
        x_ready = m.sem("x_ready")
        x2_ready = m.sem("x2_ready")
        sq_ready = m.sem("sq_ready")
        sq2_ready = m.sem("sq2_ready")
        var_ready = m.sem("var_ready")
        var2_ready = m.sem("var2_ready")
        log_done = m.sem("log_done")
        log2_done = m.sem("log2_done")
        rstd_ready = m.sem("rstd_ready")
        rstd2_ready = m.sem("rstd2_ready")
        s1_done = m.sem("s1_done")
        z2_done = m.sem("z2_done")
        z3_done = m.sem("z3_done")
        y_done = m.sem("y_done")
        hid_ready = m.sem("hid_ready")
        hid_exp = m.sem("hid_exp")
        hid_step = m.sem("hid_step")
        hid_done = m.sem("hid_done")
        att_ready = m.sem("att_ready")
        att_exp = m.sem("att_exp")
        att_step = m.sem("att_step")
        x1_done = m.sem("x1_done")

        def rows(j):
            return slice(j * CH, (j + 1) * CH)

        def two(ap):
            return ap.rearrange("p (b f) -> p b f", b=2)

        def run(eng, prepare, slot):
            with eng.Fori(0, NQ) as q:
                base = q * imgs
                prepare(q, base)
                slot(base, None, 0)
                with eng.Fori(0, (imgs - 2) // 2) as i:
                    slot(base + i * 2 + 1, base + i * 2, 1)
                    slot(base + i * 2 + 2, base + i * 2 + 1, 0)
                slot(base + (imgs - 1), base + (imgs - 2), 1)
                slot(None, base + (imgs - 1), 0)

        def j_ring(parity, j):
            return (parity * NCH + j) % 2

        def second(mi, prev, j):
            if j == 0:
                return None if prev is None else prev * NCH + (NCH - 1)
            return None if mi is None else mi * NCH + (j - 1)

        m.start()
        nc_block = ctx.enter_context(nc.Block())

        @nc_block.sync
        def _(sp):
            for tile, name in ((center, "center"), (mean, "mean"), (vec, "gate_vec"), (ca1, "ca_w1"), (ca2, "ca_w2"), (cab1, "ca_b1")):
                sp.dma_start(tile[tuple([slice(None)] * len(tile.shape))], d[name]).then_inc(w_in, 16)

            def slot(mi, prev, parity):
                half = None if mi is None else sp.snap(mi // 2)
                if mi is not None:
                    sp_wait(sp, passed, (y_done, ONE + NCH * (mi if prev is None else mi - 1)))
                    for t, o in ((ycol, 0), (yrow, 1)):
                        sp.dma_start(t[parity][:, :], d["y"][o, ds(mi * C, C), :]).then_inc(y_in[parity], 16)
                    sp.dma_start(a[parity][:, :], d["a"][ds(mi * C, C), :]).then_inc(a_in[parity], 16)
                    sp_wait(sp, passed, (x_out[parity], ONE + 16 * half))
                    sp.dma_start(x[parity][:, :], d["x_flat"][ds(mi * C, C), :]).then_inc(x_in[parity], 16)
                if prev is not None:
                    sp_wait(sp, passed, (x1_done, ONE + prev + 1))
                    sp.dma_start(d["x1"][ds(prev * C, C), :], x[1 - parity][:, :]).then_inc(x_out[1 - parity], 16)

            run(sp, lambda *_: None, slot)
            for i in range(2):
                sp_wait(sp, passed, (x_out[i], ONE + 16 * NQ * imgs // 2))

        @nc_block.gpsimd
        def _(pool):
            def slot(mi, prev, parity):
                if mi is None:
                    return
                pool.wait_ge(y_in[parity], ONE + 32 * (mi // 2 + 1))
                for j in range(NCH):
                    k = mi * NCH + j
                    if prev is not None or j >= 2:
                        pool.wait_ge(x_ready, ONE + k - 1)
                    else:
                        pool.wait_ge(x_ready, ONE + mi * NCH)
                    col = ycol[parity][:, :].rearrange("p (w h) -> p h w", w=HQ)[:, j * CROWS:(j + 1) * CROWS, :]
                    row = yrow[parity][:, rows(j)].rearrange("p (h w) -> p h w", w=HQ)
                    pool.tensor_tensor(ysum[:, j_ring(parity, j), :].rearrange("p (h w) -> p h w", w=HQ), row, col, ALU.add).then_inc(ysum_done, 1)

            run(pool, lambda *_: None, slot)

        @nc_block.tensor
        def _(pe):
            def prepare(q, base):
                pe.wait_ge(prep_raw, ONE + q + 1)
                pe.matmul(ps_t[:, 0:1], center[:, :], cur[:, 1:2], start=True, stop=True).then_inc(prep_cb, 1)
                pe.wait_ge(prep_done, ONE + q + 1)

            def product(dst, w, src, sem):
                for b in range(2):
                    mm = pe.matmul(dst[:, b, 0:HALF], w[:, :], src[:, b * HALF:(b + 1) * HALF], start=True, stop=True)
                mm.then_inc(sem, 1)

            def slot(mi, prev, parity):
                for j in range(NCH):
                    if mi is not None:
                        k = mi * NCH + j
                        pe.wait_ge(ysum_done, ONE + k + 1)
                        pe.wait_ge(s1_done, ONE + k)
                        product(ps_x, center, ysum[:, j_ring(parity, j), :], x_ready)
                    p = second(mi, prev, j)
                    if p is not None:
                        pe.wait_ge(s1_done, ONE + p + 1)
                        pe.wait_ge(z2_done, ONE + p)
                        product(ps_x2, cg, s1, x2_ready)
                    if j == 1 and prev is not None:
                        pe.wait_ge(y_done, ONE + NCH * (prev + 1))
                        for c in range(NCH):
                            mm = pe.matmul(ps_t[0:CR, 0:1], wa1[:, :], total[1 - parity][:, c:c + 1], start=(c == 0), stop=(c == NCH - 1))
                        mm.then_inc(hid_ready, 1)
                    if mi is not None:
                        pe.wait_ge(sq_ready, ONE + k + 1)
                        pe.wait_ge(log2_done, ONE + (k - 1 if prev is not None or j > 0 else k))
                        product(ps_v, mean, sq, var_ready)
                    if p is not None:
                        pe.wait_ge(sq2_ready, ONE + p + 1)
                        pe.wait_ge(log_done, ONE + (p + 2 if mi is not None else p + 1))
                        product(ps_v, mean, sq2, var2_ready)
                    if j == 1 and prev is not None:
                        pe.wait_ge(hid_done, ONE + prev + 1)
                        pe.matmul(ps_t[:, 0:1], wa2[:, :], hid[:, 4:5], start=True, stop=True).then_inc(att_ready, 1)

            run(pe, prepare, slot)

        @nc_block.scalar
        def _(act):
            def prepare(q, base):
                act.wait_ge(prep_done, ONE + q + 1)

            def slot(mi, prev, parity):
                for j in range(NCH):
                    p = second(mi, prev, j)
                    if mi is not None:
                        k = mi * NCH + j
                        act.wait_ge(x_ready, ONE + k + 1)
                        act.wait_ge(var_ready, ONE + k)
                        act.activation(two(sq[:, :]), halves(ps_x), ACT.Square).then_inc(sq_ready, 1)
                    if p is not None:
                        act.wait_ge(x2_ready, ONE + p + 1)
                        act.wait_ge(var2_ready, ONE + p)
                        act.activation(two(sq2[:, :]), halves(ps_x2), ACT.Square, bias=cb[:, 0:1]).then_inc(sq2_ready, 1)
                    if j == 1 and prev is not None:
                        act.wait_ge(hid_ready, ONE + prev + 1)
                        act.activation(hid[:, 0:1], ps_t[0:CR, 0:1], ACT.Identity, bias=ba1[:, 0:1], scale=1.0 / L).then_inc(hid_exp, 1)
                        act.wait_ge(hid_exp, ONE + 2 * prev + 1)
                        act.activation(hid[:, 1:2], hid[:, 0:1], ACT.Exp, scale=-1.0).then_inc(hid_exp, 1)
                    if j == 2 and prev is not None:
                        act.wait_ge(att_ready, ONE + prev + 1)
                        act.activation(att[:, 0:1], ps_t[:, 0:1], ACT.Identity, bias=cur[:, 4:5]).then_inc(att_exp, 1)
                        act.wait_ge(att_exp, ONE + 2 * prev + 1)
                        act.activation(att[:, 1:2], att[:, 0:1], ACT.Exp, scale=-1.0).then_inc(att_exp, 1)
                    if mi is not None:
                        act.wait_ge(var_ready, ONE + k + 1)
                        act.activation(two(logv[:, :]), halves(ps_v), ACT.Ln, bias=eps[:, 0:1]).then_inc(log_done, 1)
                        act.wait_ge(log_done, ONE + k + 1)
                        act.wait_ge(s1_done, ONE + k)
                        act.activation(rstd[:, :], logv[:, :], ACT.Exp, scale=-0.5).then_inc(rstd_ready, 1)
                    if p is not None:
                        act.wait_ge(var2_ready, ONE + p + 1)
                        act.activation(two(logv2[:, :]), halves(ps_v), ACT.Ln, bias=eps[:, 0:1]).then_inc(log2_done, 1)
                        act.wait_ge(log2_done, ONE + p + 1)
                        act.wait_ge(z2_done, ONE + p)
                        act.activation(rstd2[:, :], logv2[:, :], ACT.Exp, scale=-0.5).then_inc(rstd2_ready, 1)

            act.preload_act_table_set(LN_EXP)
            act.wait_ge(eps_set, ONE + 1)
            run(act, prepare, slot)

        @nc_block.vector
        def _(dve):
            def prepare(q, base):
                dve.wait_ge(x1_done, ONE + base)
                dve.wait_ge(x_ready, ONE + base * NCH)
                for dst, src in ((cur, vec), (wa1, ca1), (wa2, ca2)):
                    dve.tensor_copy(dst[:, :], src[:, ds(q, 1), :].rearrange("p a v -> p (a v)"))
                dve.tensor_copy(ba1[:, :], cab1[:, ds(q, 1)]).then_inc(prep_raw, 1)
                dve.wait_ge(prep_raw, ONE + q + 1)
                dve.tensor_scalar(cg[:, :], center[:, :], cur[:, 0:1], None, ALU.mult)
                dve.wait_ge(prep_cb, ONE + q + 1)
                dve.tensor_copy(cb[:, :], ps_t[:, 0:1]).then_inc(prep_done, 1)

            def slot(mi, prev, parity):
                for j in range(NCH):
                    p = second(mi, prev, j)
                    if mi is not None:
                        k = mi * NCH + j
                        dve.wait_ge(rstd_ready, ONE + k + 1)
                        if p is not None:
                            dve.wait_ge(x2_ready, ONE + p + 1)
                        dve.tensor_tensor(two(s1[:, :]), halves(ps_x), two(rstd[:, :]), ALU.mult).then_inc(s1_done, 1)
                    if j == 1 and prev is not None:
                        dve.wait_ge(hid_exp, ONE + 2 * (prev + 1))
                        dve.tensor_scalar(hid[:, 2:3], hid[:, 1:2], 1.0, None, ALU.add).then_inc(hid_step, 1)
                        dve.wait_ge(hid_step, ONE + 2 * prev + 1)
                        dve.reciprocal(hid[:, 3:4], hid[:, 2:3]).then_inc(hid_step, 1)
                        dve.wait_ge(hid_step, ONE + 2 * prev + 2)
                        dve.tensor_tensor(hid[:, 4:5], hid[:, 3:4], hid[:, 0:1], ALU.mult).then_inc(hid_done, 1)
                    if p is not None:
                        pj = (j - 1) % NCH
                        par = 1 - parity if j == 0 else parity
                        image = prev if j == 0 else mi
                        dve.wait_ge(rstd2_ready, ONE + p + 1)
                        dve.scalar_tensor_tensor(out=two(z2[:, :]), in0=halves(ps_x2), scalar=cb[:, 0:1], in1=two(rstd2[:, :]),
                                                 op0=ALU.add, op1=ALU.mult).then_inc(z2_done, 1)
                        dve.wait_ge(z2_done, ONE + p + 1)
                        dve.tensor_scalar(z3[:, :], z2[:, :], cur[:, 2:3], cur[:, 3:4], ALU.mult, ALU.add).then_inc(z3_done, 1)
                        dve.wait_ge(z3_done, ONE + p + 1)
                        dve.wait_ge(a_in[par], ONE + 16 * (image // 2 + 1))
                        dve.scalar_tensor_tensor(out=y[par][:, rows(pj)], in0=z3[:, :], scalar=1.0, in1=a[par][:, rows(pj)],
                                                 op0=ALU.mult, op1=ALU.mult, accum_out=total[par][:, pj:pj + 1]).then_inc(y_done, 1)
                    if j == 2 and prev is not None:
                        dve.wait_ge(att_exp, ONE + 2 * (prev + 1))
                        dve.tensor_scalar(att[:, 2:3], att[:, 1:2], 1.0, None, ALU.add).then_inc(att_step, 1)
                        dve.wait_ge(att_step, ONE + 2 * prev + 1)
                        dve.reciprocal(att[:, 3:4], att[:, 2:3]).then_inc(att_step, 1)
                        dve.wait_ge(att_step, ONE + 2 * prev + 2)
                        dve.wait_ge(x_in[1 - parity], ONE + 16 * (prev // 2 + 1))
                        xt = x[1 - parity][:, :]
                        dve.scalar_tensor_tensor(out=xt, in0=y[1 - parity][:, :], scalar=att[:, 3:4], in1=xt,
                                                 op0=ALU.mult, op1=ALU.add).then_inc(x1_done, 1)

            dve.memset(eps[:, :], LN_EPS).then_inc(eps_set, 1)
            dve.wait_ge(w_in, ONE + 16 * 6)
            run(dve, prepare, slot)

def residual_phase(nc, d):
    M = 576
    S = 2 * HQ
    ROWS = 16
    HT = ROWS + 2
    SUBS = 2
    SR = ROWS // SUBS
    SC = SR * S
    BR = SR // 2
    imgs = d["x"].shape[1]
    TAPS = [(dy, dx) for dy in range(3) for dx in range(3)]
    PE_TAPS, POOL_TAPS = [0], [1, 2]
    DVE_TAPS = [t for t in range(9) if t not in PE_TAPS + POOL_TAPS]
    PAIRS = S // ROWS // 2
    JOBS_PAIR = 9
    JOBS_IMG = PAIRS * JOBS_PAIR
    JOBS = 2 * JOBS_IMG
    PIECES = ROWS // BR
    CREDIT = 8

    with ExitStack() as ctx:
        m = Memory(nc, ctx, "res")
        x = [m.sbuf(f"x{i}", [C, NQ, HQ, HQ]) for i in range(2)]
        w1 = m.sbuf("w1", [C, M])
        w3 = m.sbuf("w3", [C, M])
        w3s = m.sbuf("w3s", [128, 5, C])
        wd = m.sbuf("wd", [128, 5, 9])
        bn = m.sbuf("bn", [128, 5, 8])
        bn3 = m.sbuf("bn3", [C, 4])
        sc = m.sbuf("sc", [128, 5, 2])
        bi = m.sbuf("bi", [128, 5, 2])
        sc3 = m.sbuf("sc3", [C, 1])
        bi3 = m.sbuf("bi3", [C, 1])
        eps = m.sbuf("eps", [128, 1])
        ident = m.sbuf("ident", [128, 128])
        diag = m.sbuf("diag", [128, 5, len(PE_TAPS), 128])
        diag3 = m.sbuf("diag3", [C, C])
        zeros = m.sbuf("zeros", [128, S])
        hid = [m.sbuf(f"hid{i}", [128, HT, S + 2]) for i in range(2)]
        acc = m.sbuf("acc", [128, 2, SC])
        prod = m.sbuf("prod", [128, SUBS, len(POOL_TAPS), SC])
        deep = m.sbuf("deep", [128, JOBS_PAIR, ROWS * S])
        out = m.sbuf("out", [C, 2, ROWS, S])
        ps_e = m.psum("ps_e", [128, 2, BANK])
        ps_t = m.psum("ps_t", [128, 2, 2, BANK])
        ps_o = m.psum("ps_o", [C, 2, BANK])

        w_in = m.sem("w_in")
        passed = m.sem("passed")
        x_in = [m.sem(f"x_in{i}") for i in range(2)]
        out_out = [m.sem(f"out_out{i}") for i in range(2)]
        cleared = m.sem("cleared")
        bn_log = m.sem("bn_log")
        bn_rs = m.sem("bn_rs")
        bn_scale = m.sem("bn_scale")
        bn_shift = m.sem("bn_shift")
        w3_ready = m.sem("w3_ready")
        prep_done = m.sem("prep_done")
        exp_ready = m.sem("exp_ready")
        hid_done = m.sem("hid_done")
        taps_ready = m.sem("taps_ready")
        dve_tap = m.sem("dve_tap")
        dve_done = m.sem("dve_done")
        prod_ready = m.sem("prod_ready")
        pool_mid = m.sem("pool_mid")
        pool_done = m.sem("pool_done")
        deep_done = m.sem("deep_done")
        proj_ready = m.sem("proj_ready")
        out_done = m.sem("out_done")

        def job(i):
            img, rest = divmod(i, JOBS_IMG)
            pair, k = divmod(rest, JOBS_PAIR)
            return img, pair, k, (k if k < 4 else 4 if k == 4 else k - 5)

        def strips_of(pair, k):
            if k < 4:
                return [(pair, 0, 128)]
            if k == 4:
                return [(pair, 0, 64), (pair + PAIRS, 64, 64)]
            return [(pair + PAIRS, 0, 128)]

        def runs(first, n):
            found = []
            for r in range(first, first + n):
                c = min(max(r, 0), S - 1)
                last = found[-1] if found else None
                if last and last[1] + last[2] == c and c != HQ and c == r and last[3]:
                    last[2] += 1
                else:
                    found.append([r - first, c, 1, c == r])
            return [(at, c, k) for at, c, k, _ in found]

        def pieces_after(i):
            img, pair, k, _ = job(i)
            if 5 <= k:
                return [(img, pair, 0, k - 5)]
            if k < 4:
                if pair > 0:
                    return [(img, pair - 1, 1, k)]
                if img == 1:
                    return [(0, PAIRS - 1, 1, k)]
            return []

        all_pieces = []
        after = []
        for i in range(JOBS):
            after.append(pieces_after(i))
            all_pieces += after[-1]
        drain = [(1, PAIRS - 1, 1, g) for g in range(PIECES)]
        all_pieces += drain
        NPIECE = len(all_pieces)
        number = {p: n for n, p in enumerate(all_pieces)}
        NSTRIP = NPIECE // PIECES

        edge_written = m.sem("edge_written")

        def edge_jobs():
            found = []
            for i in range(1, JOBS + 1):
                img, pair, k, t = job(i % JOBS)
                for rnd in range(2):
                    for strip, p0, np_ in strips_of(pair, k):
                        if (strip == 0 and rnd == 0) or (strip == 2 * PAIRS - 1 and rnd == 1):
                            found.append((i, rnd))
            return found

        edges = len(edge_jobs())

        def edge_count(i, rnd):
            if i == 0:
                return 1
            return 2 + edge_jobs().index((i, rnd))

        def pieces_before(i):
            img, pair, k, t = job(i)
            g = img * PAIRS + pair - 1
            if g < 0:
                return 0
            pimg, ppair = divmod(g, PAIRS)
            b = 0 if k < 4 else 1
            return number[(pimg, ppair, b, PIECES - 1)] + 1

        def ps_o_w(t):
            return ps_t[:, t // 4, 0, (t % 4) * C:(t % 4 + 1) * C]

        m.start()
        nc_block = ctx.enter_context(nc.Block())

        @nc_block.sync
        def _(sp):
            for tile, name in ((w1, "w1"), (w3, "w3"), (wd, "wd"), (bn, "bn"), (bn3, "bn3"), (ident, "ident")):
                sp.dma_start(tile[tuple([slice(None)] * len(tile.shape))], d[name]).then_inc(w_in, 16)

            def load(parity, image):
                sp.dma_start(x[parity][:, :, :, :].rearrange("c q h w -> c q (h w)"),
                             d["x1_img"][:, ds(image, 1), :, :].rearrange("q b c l -> c (b q) l")).then_inc(x_in[parity], 16)

            load(0, 0)
            with sp.Fori(0, imgs // 2) as it:
                after_next = sp.snap((it * 2 + 2) % imgs)
                sp_wait(sp, passed, (out_done, ONE + CREDIT + it * NPIECE))
                load(1, it * 2 + 1)
                done = 0
                for n, (img, pair, b, g) in enumerate(all_pieces):
                    if g < PIECES - 1:
                        continue
                    sp_wait(sp, passed, (out_done, ONE + CREDIT + it * NPIECE + (n + 1)))
                    strip = pair + b * PAIRS
                    par = (n // PIECES) % 2
                    sp.dma_start(d["out"][ds(it * 2 + img, 1), :, strip * ROWS:(strip + 1) * ROWS, :]
                                 .rearrange("a c h w -> (a c) h w"), out[:, par, :, :]).then_inc(out_out[par], 16)
                    if (img, pair, b) == (0, PAIRS - 1, 1):
                        load(0, after_next)
            for i in range(2):
                sp_wait(sp, passed, (out_out[i], ONE + 16 * (NSTRIP // 2) * (imgs // 2)))
            sp_wait(sp, passed, (x_in[0], ONE + 16 * (imgs // 2 + 1)))

        @nc_block.tensor
        def _(pe):
            def expand(it, i):
                img, pair, k, t = job(i % JOBS)
                nxt = i // JOBS
                pe.wait_ge(x_in[img], ONE + 16 * (it + nxt + 1))
                for rnd, (row, n) in enumerate(((0, 5), (10, 4))):
                    pe.wait_ge(hid_done, ONE + it * (2 * JOBS) + (2 * i + rnd))
                    for b in range(2):
                        for strip, p0, np_ in strips_of(pair, k):
                            for at, src, cnt in runs(strip * ROWS - 1 + row + b * n, n):
                                half, loc = divmod(src, HQ)
                                rhs = x[img][:, 2 * half:2 * half + 2, loc:loc + cnt, :].rearrange("c q r w -> c r q w")
                                dst = ps_e[p0:p0 + np_, b, at * S:(at + cnt) * S].rearrange("p (r q w) -> p r q w", q=2, w=HQ)
                                mm = pe.matmul(dst, w1[:, t * 128:t * 128 + np_], rhs, start=True, stop=True)
                    mm.then_inc(exp_ready, 1)

            def taps(it, i, sub):
                img, pair, k, t = job(i)
                u = it * (2 * JOBS) + (2 * i + sub)
                pe.wait_ge(hid_done, ONE + it * (2 * JOBS) + 2 * (i + 1))
                pe.wait_ge(dve_done, ONE + CREDIT + u - 1)
                for n, tap in enumerate(PE_TAPS):
                    dy, dx = TAPS[tap]
                    for b in range(2):
                        r = sub * SR + b * BR + dy
                        mm = pe.matmul(ps_t[:, sub, b, 0:BR * S].rearrange("p (r w) -> p r w", w=S), diag[:, t, n, :],
                                       hid[i % 2][:, r:r + BR, dx:dx + S], start=(n == 0), stop=(n == len(PE_TAPS) - 1))
                mm.then_inc(taps_ready, 1)

            def project(it, piece):
                img, pair, b, g = piece
                n = it * NPIECE + number[piece]
                last = (img * PAIRS + pair) * JOBS_PAIR + (4 if b == 0 else 8)
                pe.wait_ge(deep_done, ONE + CREDIT + it * (2 * JOBS) + 2 * (last + 1))
                pe.wait_ge(out_done, ONE + CREDIT + n - 1)
                cols = slice(g * BR * S, (g + 1) * BR * S)
                dst = ps_o[:, number[piece] % 2, 0:BR * S]
                for t in range(4):
                    pe.matmul(dst, w3s[:, t, :], deep[:, 5 * b + t, cols], start=(t == 0), stop=False)
                p0 = 64 * b
                pe.matmul(dst, w3s[p0:p0 + 64, 4, :], deep[p0:p0 + 64, 4, cols], start=False, stop=True).then_inc(proj_ready, 1)

            pe.wait_ge(bn_shift, ONE + 3)
            for t in range(5):
                n = 128 if t < 4 else 64
                for p0 in ([0] if t < 4 else [0, 64]):
                    bank, at = (0, t) if t < 4 else (1, 0)
                    mm = pe.matmul(ps_o_w(t)[p0:p0 + n, :], w3[:, t * 128:t * 128 + n], diag3[:, :], start=True, stop=True)
            mm.then_inc(w3_ready, 1)
            pe.wait_ge(prep_done, ONE + 1)
            expand(0, 0)
            with pe.Fori(0, imgs // 2) as it:
                for i in range(JOBS):
                    taps(it, i, 0)
                    expand(it, i + 1)
                    taps(it, i, 1)
                    for piece in after[i]:
                        project(it, piece)
                for piece in drain:
                    project(it, piece)

        @nc_block.scalar
        def _(act):
            def evac(it, i, rnd):
                img, pair, k, t = job(i % JOBS)
                e = it * (2 * JOBS) + (2 * i + rnd)
                row, n = ((0, 5), (10, 4))[rnd]
                act.wait_ge(exp_ready, ONE + e + 1)
                act.wait_ge(dve_done, ONE + CREDIT + it * (2 * JOBS) + 2 * (i - 1))
                if i > 0:
                    act.wait_ge(prod_ready, ONE + it * (2 * JOBS) + 2 * (i - 1))
                dst = hid[i % 2][:, row:row + 2 * n, 1:1 + S].rearrange("p (b r) w -> p b r w", b=2)
                src = ps_e[:, :, 0:n * S].rearrange("p b (r w) -> p b r w", w=S)
                ins = act.activation(dst, src, ACT.Relu, bias=bi[:, t, 0:1], scale=sc[:, t, 0:1])
                for strip, p0, np_ in strips_of(pair, k):
                    edge = 0 if strip == 0 and rnd == 0 else HT - 1 if strip == 2 * PAIRS - 1 and rnd == 1 else None
                    if edge is not None:
                        ins.then_inc(edge_written, 1)
                        act.wait_ge(edge_written, ONE + it * edges + edge_count(i, rnd))
                        ins = act.activation(hid[i % 2][p0:p0 + np_, edge, 1:1 + S], zeros[p0:p0 + np_, :], ACT.Copy)
                ins.then_inc(hid_done, 1)

            def products(it, i, sub):
                img, pair, k, t = job(i)
                u = it * (2 * JOBS) + (2 * i + sub)
                act.wait_ge(hid_done, ONE + it * (2 * JOBS) + 2 * (i + 1))
                act.wait_ge(pool_done, ONE + CREDIT + u - 1)
                for n, tap in enumerate(POOL_TAPS):
                    dy, dx = TAPS[tap]
                    r = sub * SR + dy
                    ins = act.activation(prod[:, sub, n, :].rearrange("p (r w) -> p r w", w=S), hid[i % 2][:, r:r + SR, dx:dx + S],
                                         ACT.Copy, scale=wd[:, t, tap:tap + 1])
                ins.then_inc(prod_ready, 1)

            def deepen(it, i, sub):
                img, pair, k, t = job(i)
                u = it * (2 * JOBS) + (2 * i + sub)
                act.wait_ge(pool_done, ONE + CREDIT + u + 1)
                if sub == 0:
                    n = pieces_before(i)
                    act.wait_ge(proj_ready, ONE + it * NPIECE + n)
                act.activation(deep[:, k, sub * SC:(sub + 1) * SC], acc[:, sub, :], ACT.Relu, bias=bi[:, t, 1:2],
                               scale=sc[:, t, 1:2]).then_inc(deep_done, 1)

            act.preload_act_table_set(LN_EXP)
            act.wait_ge(w_in, ONE + 16 * 6)
            act.wait_ge(cleared, ONE + 4)
            act.activation(sc[:, :, 0], bn[:, :, 3], ACT.Ln, bias=eps[:, 0:1])
            act.activation(sc[:, :, 1], bn[:, :, 7], ACT.Ln, bias=eps[:, 0:1])
            act.activation(sc3[:, :], bn3[:, 3:4], ACT.Ln, bias=eps[0:C, 0:1]).then_inc(bn_log, 1)
            act.wait_ge(bn_log, ONE + 1)
            act.activation(sc[:, :, :], sc[:, :, :], ACT.Exp, scale=-0.5)
            act.activation(sc3[:, :], sc3[:, :], ACT.Exp, scale=-0.5).then_inc(bn_rs, 1)
            act.wait_ge(bn_shift, ONE + 3)
            evac(0, 0, 0)
            evac(0, 0, 1)
            with act.Fori(0, imgs // 2) as it:
                for i in range(JOBS):
                    products(it, i, 0)
                    evac(it, i + 1, 0)
                    if i > 0:
                        deepen(it, i - 1, 1)
                    evac(it, i + 1, 1)
                    products(it, i, 1)
                    deepen(it, i, 0)
                deepen(it, JOBS - 1, 1)

        @nc_block.vector
        def _(dve):
            def depthwise(it, i, sub):
                img, pair, k, t = job(i)
                u = it * (2 * JOBS) + (2 * i + sub)
                dve.wait_ge(hid_done, ONE + it * (2 * JOBS) + 2 * (i + 1))
                dve.wait_ge(taps_ready, ONE + u + 1)
                psum = ps_t[:, sub, :, 0:BR * S].rearrange("p b (r w) -> p b r w", w=S)
                for n, tap in enumerate(DVE_TAPS):
                    dy, dx = TAPS[tap]
                    r = sub * SR + dy
                    src = hid[i % 2][:, r:r + SR, dx:dx + S].rearrange("p (b r) w -> p b r w", b=2)
                    last = n == len(DVE_TAPS) - 1
                    if n:
                        dve.wait_ge(dve_tap, ONE + u * (len(DVE_TAPS) - 1) + n)
                    if last:
                        dve.wait_ge(deep_done, ONE + CREDIT + u - 1)
                    dst = acc[:, sub, :].rearrange("p (b r w) -> p b r w", b=2, w=S) if last else psum
                    dve.scalar_tensor_tensor(out=dst, in0=src, scalar=wd[:, t, tap:tap + 1], in1=psum,
                                             op0=ALU.mult, op1=ALU.add).then_inc(dve_done if last else dve_tap, 1)

            def residual(it, piece):
                img, pair, b, g = piece
                num = number[piece]
                dve.wait_ge(proj_ready, ONE + it * NPIECE + num + 1)
                strip = num // PIECES
                if g == 0:
                    dve.wait_ge(out_out[strip % 2], ONE + 16 * (it * (NSTRIP // 2) + strip // 2))
                row = (pair + b * PAIRS) * ROWS + g * BR
                half, loc = divmod(row, HQ)
                for q in range(2):
                    src = ps_o[:, num % 2, 0:BR * S].rearrange("p (r q w) -> p r q w", q=2, w=HQ)[:, :, q, :]
                    ins = dve.scalar_tensor_tensor(out=out[:, strip % 2, g * BR:(g + 1) * BR, q * HQ:(q + 1) * HQ], in0=src,
                                                   scalar=bi3[:, 0:1], in1=x[img][:, 2 * half + q, loc:loc + BR, :],
                                                   op0=ALU.add, op1=ALU.add)
                ins.then_inc(out_done, 1)

            for i in range(2):
                dve.memset(hid[i][:, :, :], 0.0).then_inc(cleared, 1)
            dve.memset(zeros[:, :], 0.0).then_inc(cleared, 1)
            dve.memset(eps[:, :], BN_EPS).then_inc(cleared, 1)
            dve.memset(acc[:, 0, 0:1], 0.0).then_inc(dve_done, CREDIT)
            dve.memset(acc[:, 0, 1:2], 0.0).then_inc(out_done, CREDIT)
            dve.memset(acc[:, 0, 3:4], 0.0).then_inc(deep_done, CREDIT)
            dve.wait_ge(w_in, ONE + 16 * 6)
            dve.wait_ge(bn_rs, ONE + 1)
            dve.tensor_tensor(sc[:, :, 0], sc[:, :, 0], bn[:, :, 0], ALU.mult)
            dve.tensor_tensor(sc[:, :, 1], sc[:, :, 1], bn[:, :, 4], ALU.mult)
            dve.tensor_tensor(sc3[:, :], sc3[:, :], bn3[:, 0:1], ALU.mult).then_inc(bn_scale, 1)
            dve.wait_ge(bn_scale, ONE + 1)
            dve.tensor_tensor(bi[:, :, 0], sc[:, :, 0], bn[:, :, 2], ALU.mult)
            dve.tensor_tensor(bi[:, :, 1], sc[:, :, 1], bn[:, :, 6], ALU.mult)
            dve.tensor_tensor(bi3[:, :], sc3[:, :], bn3[:, 2:3], ALU.mult)
            dve.tensor_scalar(diag3[:, :], ident[0:C, 0:C], sc3[:, 0:1], None, ALU.mult)
            for t in range(5):
                for n, tap in enumerate(PE_TAPS):
                    dve.tensor_scalar(diag[:, t, n, :], ident[:, :], wd[:, t, tap:tap + 1], None, ALU.mult)
            dve.memset(acc[:, 0, 2:3], 0.0).then_inc(bn_scale, 1)
            dve.wait_ge(bn_scale, ONE + 2)
            dve.tensor_tensor(bi[:, :, 0], bn[:, :, 1], bi[:, :, 0], ALU.subtract).then_inc(bn_shift, 1)
            dve.tensor_tensor(bi[:, :, 1], bn[:, :, 5], bi[:, :, 1], ALU.subtract).then_inc(bn_shift, 1)
            dve.tensor_tensor(bi3[:, :], bn3[:, 1:2], bi3[:, :], ALU.subtract).then_inc(bn_shift, 1)
            dve.wait_ge(w3_ready, ONE + 1)
            for t in range(5):
                ins = dve.tensor_copy(w3s[:, t, :], ps_o_w(t))
            ins.then_inc(prep_done, 1)
            with dve.Fori(0, imgs // 2) as it:
                for i in range(JOBS):
                    for sub in range(2):
                        depthwise(it, i, sub)
                    if i > 0:
                        for piece in after[i - 1]:
                            residual(it, piece)
                for piece in after[JOBS - 1] + drain:
                    residual(it, piece)

        @nc_block.gpsimd
        def _(pool):
            pool.memset(prod[:, 0, 0, 0:1], 0.0).then_inc(pool_done, CREDIT)
            with pool.Fori(0, imgs // 2) as it:
                for i in range(JOBS):
                    for sub in range(2):
                        u = it * (2 * JOBS) + (2 * i + sub)
                        pool.wait_ge(prod_ready, ONE + u + 1)
                        for n in range(1, len(POOL_TAPS)):
                            pool.tensor_tensor(prod[:, sub, 0, :], prod[:, sub, 0, :], prod[:, sub, n, :], ALU.add).then_inc(pool_mid, 1)
                            pool.wait_ge(pool_mid, ONE + u * (len(POOL_TAPS) - 1) + n)
                        pool.wait_ge(dve_done, ONE + CREDIT + u + 1)
                        pool.tensor_tensor(acc[:, sub, :], acc[:, sub, :], prod[:, sub, 0, :], ALU.add).then_inc(pool_done, 1)


def build(nc, d):
    imgs = d["x"].shape[1]
    total = NQ * imgs
    sets = total // IMGS

    def scratch(name, shape, dtype=F32):
        return nc.dram_tensor(f"scratch_{name}", shape, dtype, kind="Internal").ap()

    d["x_flat"] = d["x"].rearrange("q b c l -> (q b c) l")
    d["z"] = scratch("z", (2, total * C, L))
    d["y"] = scratch("y", (2, total * C, L))
    d["a"] = scratch("a", (total * C, L))
    d["bc"] = scratch("bc", (sets, 2, 2, 2, IMGS, PARTS * N, L), BF16)
    d["dts4"] = scratch("dts", (sets, 2, 2, IMGS, R, L))
    d["dts"] = d["dts4"].rearrange("s o r i k l -> s o r (i k) l")
    x1 = scratch("x1", (NQ, imgs, C, L))
    d["x1"] = x1.rearrange("q b c l -> (q b c) l")
    d["x1_img"] = x1
    front_phase(nc, d)
    scan_phase(nc, d)
    gate_phase(nc, d)
    residual_phase(nc, d)


def layouts(i):
    f = np.float32
    a = {}
    imgs = i["x"].shape[0]
    tiles = NQ * imgs * C // 128
    a["x"] = i["x"].reshape(imgs, C, 2, HQ, 2, HQ).transpose(2, 4, 0, 1, 3, 5).reshape(NQ, imgs, C, L)
    lead = lambda w: w.transpose(2, 0, 1)
    a["p1_w"] = lead(i["L0_conv_p1_w"])
    a["p2in_w"] = lead(i["L0_conv_p2in_w"])
    a["dw_w"] = i["L0_conv_dw_w"].reshape(NQ, C, 9).transpose(1, 0, 2)
    a["front_vec"] = np.stack([i["L0_conv_" + n].T for n in ("ln_g", "ln_b", "p1_b", "p2in_b", "dw_b")], axis=2)
    a["gate_vec"] = np.stack([i["L0_conv_" + n].T for n in ("ssln_g", "ssln_b", "p2n_g", "p2n_b", "ca_b2")], axis=2)
    a["ca_w1"] = lead(i["L0_conv_ca_w1"])
    a["ca_w2"] = lead(i["L0_conv_ca_w2"])
    a["ca_b1"] = i["L0_conv_ca_b1"].T
    xw = i["L0_conv_xproj_w"]
    wx = np.zeros((C, NQ, 2, 64), f)
    prm = np.zeros((NQ, 2, C, 2 * N + 4), f)
    for o in range(2):
        for r in range(2):
            k = o + 2 * r
            wx[:, :, o, 8 * r:8 * r + N] = xw[:, k, R:R + N].transpose(2, 0, 1)
            wx[:, :, o, 16 + 8 * r:16 + 8 * r + N] = xw[:, k, R + N:R + 2 * N].transpose(2, 0, 1)
            wx[:, :, o, 32 + R * r:32 + R * (r + 1)] = xw[:, k, 0:R].transpose(2, 0, 1)
            prm[:, o, :, r * N:(r + 1) * N] = i["L0_conv_A_logs"][:, k]
            prm[:, o, :, 2 * N + r] = i["L0_conv_Ds"][:, k]
            prm[:, o, :, 2 * N + 2 + r] = i["L0_conv_dtproj_b"][:, k]
    a["xproj_w"] = wx
    packed = np.repeat(prm[:, None], imgs, axis=1).transpose(2, 0, 1, 3, 4).reshape(2, tiles, 128, 2 * N + 4)
    a["prm"] = packed.transpose(1, 0, 2, 3)
    wdt = np.zeros((tiles, 2, IMGS * R, 2, 128), f)
    select = np.zeros((TILES, IMGS * PARTS * N, N, 128), f)
    per_q = tiles // NQ
    for t in range(TILES):
        for p in range(128):
            img, c = divmod(t * 128 + p, C)
            for n in range(N):
                select[t, [img * PARTS * N + j * N + n for j in range(PARTS)], n, p] = 1.0
            for o in range(2):
                for r in range(2):
                    for q in range(NQ):
                        wdt[q * per_q + t:(q + 1) * per_q:TILES, o, img * R:(img + 1) * R, r, p] = i["L0_conv_dtproj_w"][q, o + 2 * r, c]
    a["wdt"] = wdt
    a["select"] = select.astype(mybir.dt.np(BF16))
    a["ident"] = np.eye(128, dtype=f)
    a["mean"] = np.full((C, C), 1.0 / C, f)
    a["center"] = np.eye(C, dtype=f) - np.full((C, C), 1.0 / C, f)
    hidden = np.concatenate([np.arange(576), np.arange(512, 576)])
    a["w1"] = i["L1_conv_w1"].reshape(576, C).T
    a["w3"] = i["L1_conv_w3"].reshape(C, 576)
    a["wd"] = i["L1_conv_wd"].reshape(576, 9)[hidden].reshape(5, 128, 9).transpose(1, 0, 2)
    bn = np.stack([i["L1_conv_" + n] for n in ("g1", "b1", "m1", "v1", "g2", "b2", "m2", "v2")], axis=1)
    a["bn"] = bn[hidden].reshape(5, 128, 8).transpose(1, 0, 2)
    a["bn3"] = np.stack([i["L1_conv_" + n] for n in ("g3", "b3", "m3", "v3")], axis=1)
    return {k: np.ascontiguousarray(v) for k, v in a.items()}


def kernel(**inputs):
    import concourse.bacc as bacc
    from concourse.bass_utils import run_bass_kernel_spmd

    nc = bacc.Bacc("TRN2", target_bir_lowering=False, num_devices=1)
    inputs = {k: np.asarray(v) for k, v in inputs.items()}
    arrays = {f"in_{k}_dram": v for k, v in layouts(inputs).items()}
    d = {}
    for name, v in arrays.items():
        d[name[3:-5]] = nc.dram_tensor(name, v.shape, mybir.dt.from_np(v.dtype), kind="ExternalInput").ap()
    d["out"] = nc.dram_tensor("out_0_dram", inputs["x"].shape, F32, kind="ExternalOutput").ap()
    build(nc, d)
    r = run_bass_kernel_spmd(nc, [arrays], core_ids=[0])
    return r.results[0]["out_0_dram"]
```

```python
from contextlib import ExitStack

import numpy as np

import concourse.bass as bass
from concourse import mybir

F32 = mybir.dt.float32
BF16 = mybir.dt.bfloat16
ALU = mybir.AluOpType
ACT = mybir.ActivationFunctionType
ds = bass.ds

C = 96
HQ = 48
L = HQ * HQ
NQ = 4
N = 8
R = 6
CR = 12
IMGS = 4
TILES = IMGS * C // 128
PARTS = 3
NCH = 3
CH = L // NCH
CROWS = HQ // NCH
HALF = CH // 2
BANK = 512
LN_EPS = 1e-6
LN_EXP = "natural_log_exp_and_others"
BN_EPS = 1e-5
ONE = 1


class Memory:

    def __init__(self, nc, ctx, tag):
        self.nc, self.ctx, self.tag = nc, ctx, tag
        self.sems = []

    def sbuf(self, name, shape, dtype=F32):
        return self.ctx.enter_context(self.nc.sbuf_tensor(f"{self.tag}_{name}", shape, dtype))

    def psum(self, name, shape):
        return self.ctx.enter_context(self.nc.psum_tensor(f"{self.tag}_{name}", shape, F32))

    def sem(self, name):
        self.sems.append(self.ctx.enter_context(self.nc.semaphore(f"{self.tag}_{name}")))
        return self.sems[-1]

    def start(self):
        with self.nc.Block() as block:
            @block.sync
            def _(sp):
                for sem in self.sems:
                    sp.sem_inc(sem, ONE)


def halves(ap):
    return ap[:, :, 0:HALF]


def in_halves(ap):
    return ap.rearrange("p (b f) -> p b f", b=2)


def sp_wait(sp, passed, *pairs):
    for sem, value in pairs:
        sp.wait_ge(sem, value)
        sp.sem_inc(passed, 1)


def front_phase(nc, d):
    imgs = d["x"].shape[1]
    TAPS = [(dy, dx) for dy in range(3) for dx in range(3)]
    PE_TAPS = 2
    PAD = HQ + 2

    with ExitStack() as ctx:
        m = Memory(nc, ctx, "front")
        w1all = m.sbuf("w1all", [C, NQ, C])
        w2all = m.sbuf("w2all", [C, NQ, C])
        wxall = m.sbuf("wxall", [C, NQ, 2, 64])
        dwall = m.sbuf("dwall", [C, NQ, 9])
        vec = m.sbuf("vec", [C, NQ, 5])
        center = m.sbuf("center", [C, C])
        mean = m.sbuf("mean", [C, C])
        ident = m.sbuf("ident", [C, C])
        eps = m.sbuf("eps", [C, 1])
        w1raw = m.sbuf("w1raw", [C, C])
        w2raw = m.sbuf("w2raw", [C, C])
        w1 = m.sbuf("w1", [C, C])
        w2 = m.sbuf("w2", [C, C])
        wx = m.sbuf("wx", [C, 2, 64])
        dw = m.sbuf("dw", [C, 9])
        diag = m.sbuf("diag", [C, PE_TAPS, C])
        cur = m.sbuf("cur", [C, 5])
        bias = m.sbuf("bias", [C, 2])
        x = [m.sbuf(f"x{i}", [C, L]) for i in range(2)]
        sq = m.sbuf("sq", [C, CH])
        logv = m.sbuf("logv", [C, CH])
        rstd = m.sbuf("rstd", [C, CH])
        h = m.sbuf("h", [C, CH])
        pad = [m.sbuf(f"pad{i}", [C, PAD, PAD]) for i in range(2)]
        apre = [m.sbuf(f"apre{i}", [C, L]) for i in range(2)]
        a = m.sbuf("a", [C, L])
        zpre = [m.sbuf(f"zpre{i}", [C, L]) for i in range(2)]
        zrow = m.sbuf("zrow", [C, L])
        zcol = m.sbuf("zcol", [C, L])
        proj = [m.sbuf(f"proj{i}", [128, L]) for i in range(2)]
        rest = m.sbuf("rest", [128, CH])
        parts = [[m.sbuf(f"part{j}{i}", [128, L], BF16) for j in range(PARTS)] for i in range(2)]
        ps_x = m.psum("ps_x", [C, 2, BANK])
        ps_w = m.psum("ps_w", [C, 2, BANK])
        ps_d = m.psum("ps_d", [C, 2, BANK])
        ps_p = m.psum("ps_p", [128, 2, BANK])

        w_in = m.sem("w_in")
        passed = m.sem("passed")
        x_in = [m.sem(f"x_in{i}") for i in range(2)]
        a_out = m.sem("a_out")
        zrow_out = m.sem("zrow_out")
        zcol_out = m.sem("zcol_out")
        parts_out = [m.sem(f"parts_out{i}") for i in range(2)]
        prep_raw = m.sem("prep_raw")
        prep_fold = m.sem("prep_fold")
        prep_bias = m.sem("prep_bias")
        prep_done = m.sem("prep_done")
        pads_zeroed = m.sem("pads_zeroed")
        xc_ready = m.sem("xc_ready")
        sq_ready = m.sem("sq_ready")
        var_ready = m.sem("var_ready")
        log_done = m.sem("log_done")
        rstd_ready = m.sem("rstd_ready")
        h_done = m.sem("h_done")
        conv1_ready = m.sem("conv1_ready")
        conv2_ready = m.sem("conv2_ready")
        apre_done = m.sem("apre_done")
        pad_done = m.sem("pad_done")
        a_done = m.sem("a_done")
        taps_ready = m.sem("taps_ready")
        taps_taken = m.sem("taps_taken")
        dve_tap = m.sem("dve_tap")
        zpre_done = m.sem("zpre_done")
        zrow_done = m.sem("zrow_done")
        zcol_done = m.sem("zcol_done")
        proj_ready = m.sem("proj_ready")
        proj_copied = m.sem("proj_copied")
        rest_done = m.sem("rest_done")
        mid_done = m.sem("mid_done")
        parts_done = m.sem("parts_done")

        DVE_TAPS = len(TAPS) - PE_TAPS

        def rows(j):
            return slice(j * CH, (j + 1) * CH)

        def window(buf, j, tap):
            dy, dx = TAPS[tap]
            return buf[:, j * CROWS + dy:(j + 1) * CROWS + dy, dx:dx + HQ].rearrange("p (b r) w -> p b r w", b=2)

        def image(ps):
            return ps[:, :, 0:HALF].rearrange("p b (r w) -> p b r w", w=HQ)

        def run(eng, prepare, slot):
            with eng.Fori(0, NQ) as q:
                base = q * imgs
                last = base + (imgs - 1)
                pair = q * (imgs // 2)
                prepare(q)
                slot(base, None, None, None, 0, None)
                slot(base + 1, base, None, None, 1, None)
                slot(base + 2, base + 1, base, None, 0, pair)
                slot(base + 3, base + 2, base + 1, base, 1, pair)
                if imgs > 4:
                    with eng.Fori(0, (imgs - 4) // 2) as i:
                        two = base + i * 2
                        slot(two + 4, two + 3, two + 2, two + 1, 0, pair + i + 1)
                        slot(two + 5, two + 4, two + 3, two + 2, 1, pair + i + 1)
                slot(None, last, last - 1, last - 2, 0, pair + (imgs // 2 - 1))
                slot(None, None, last, last - 1, 1, pair + (imgs // 2 - 1))
                slot(None, None, None, last, 0, None)

        def lagging(mf, mb, parity, j):
            if j == 0:
                return None if mb is None else (mb, NCH - 1, 1 - parity)
            return None if mf is None else (mf, j - 1, parity)

        def projected(mp, mq, parity, j):
            if j == 0:
                return None if mq is None else (mq, NCH - 1, 1 - parity)
            return None if mp is None else (mp, j - 1, parity)

        nothing = lambda *_: None
        total = NQ * imgs
        m.start()
        nc_block = ctx.enter_context(nc.Block())

        @nc_block.sync
        def _(sp):
            loads = [(w1all, "p1_w"), (w2all, "p2in_w"), (wxall, "xproj_w"), (dwall, "dw_w"), (vec, "front_vec"),
                     (center, "center"), (mean, "mean"), (ident, "ident")]
            for tile, name in loads:
                src = d[name] if name != "ident" else d[name][0:C, 0:C]
                sp.dma_start(tile[tuple([slice(None)] * len(tile.shape))], src).then_inc(w_in, 16)

            def load_x(mi, parity):
                sp.dma_start(x[parity][:, :], d["x_flat"][ds(mi * C, C), :]).then_inc(x_in[parity], 16)

            def slot(mf, mb, mp, mq, parity, pair):
                after = None if mf is None else sp.snap((mf + 1) % total)
                place = None if mq is None else (sp.snap(mq // IMGS), sp.snap(mq % IMGS))
                if mf is not None:
                    sp_wait(sp, passed, (xc_ready, ONE + mf * NCH))
                    load_x(after, 1 - parity)
                if mq is not None:
                    sp_wait(sp, passed, (parts_done, ONE + NCH * (mq + 1)), (proj_copied, ONE + 2 * NCH * (mq + 1)))
                    st, im = place
                    for o in range(2):
                        for j in range(PARTS):
                            for k in range(2):
                                for r in range(2):
                                    lo = 64 * o + 16 * k + 8 * r
                                    sp.dma_start(d["bc"][ds(st, 1), o, k, r, ds(im, 1), N * j:N * (j + 1), :]
                                                 .rearrange("s i n l -> (s i n) l"),
                                                 parts[1 - parity][j][lo:lo + N, :]).then_inc(parts_out[1 - parity], 16)
                        for r in range(2):
                            lo = 64 * o + 32 + R * r
                            sp.dma_start(d["dts4"][ds(st, 1), o, r, ds(im, 1), :, :].rearrange("s i k l -> (s i k) l"),
                                         proj[1 - parity][lo:lo + R, :]).then_inc(parts_out[1 - parity], 16)
                if mp is not None:
                    sp_wait(sp, passed, (zrow_done, ONE + mp + 1))
                    sp.dma_start(d["z"][1, ds(mp * C, C), :], zrow[:, :]).then_inc(zrow_out, 16)
                    sp_wait(sp, passed, (zcol_done, ONE + mp + 1))
                    sp.dma_start(d["z"][0, ds(mp * C, C), :], zcol[:, :]).then_inc(zcol_out, 16)
                    sp_wait(sp, passed, (a_done, ONE + mp + 1))
                    sp.dma_start(d["a"][ds(mp * C, C), :], a[:, :]).then_inc(a_out, 16)

            load_x(0, 0)
            run(sp, nothing, slot)
            sp_wait(sp, passed, (x_in[0], ONE + 16 * (total // 2 + 1)))
            for sem, n in ((a_out, total), (zrow_out, total), (zcol_out, total), (parts_out[0], total * 14), (parts_out[1], total * 14)):
                sp_wait(sp, passed, (sem, ONE + 16 * n))

        @nc_block.tensor
        def _(pe):
            def prepare(q):
                pe.wait_ge(prep_raw, ONE + q + 1)
                pe.matmul(ps_w[:, 0, 0:1], w1raw[:, :], cur[:, 1:2], start=True, stop=True)
                pe.matmul(ps_w[:, 1, 0:1], w2raw[:, :], cur[:, 1:2], start=True, stop=True).then_inc(prep_bias, 1)
                pe.wait_ge(prep_done, ONE + q + 1)

            def front(mi, j, parity):
                k = mi * NCH + j
                pe.wait_ge(x_in[parity], ONE + 16 * (mi // 2 + 1))
                pe.wait_ge(h_done, ONE + k)
                for b in range(2):
                    mm = pe.matmul(ps_x[:, b, 0:HALF], center[:, :], x[parity][:, j * CH + b * HALF:j * CH + (b + 1) * HALF], start=True, stop=True)
                mm.then_inc(xc_ready, 1)

            def variance(mi, j, mp, mq):
                k = mi * NCH + j
                pe.wait_ge(sq_ready, ONE + k + 1)
                if j < 2 and mq is not None:
                    pe.wait_ge(proj_copied, ONE + 2 * (mq * NCH + 2 + j))
                if j == 2 and mp is not None:
                    pe.wait_ge(proj_copied, ONE + 2 * (mp * NCH + 1))
                for b in range(2):
                    mm = pe.matmul(ps_p[0:C, b, 0:HALF], mean[:, :], sq[:, b * HALF:(b + 1) * HALF], start=True, stop=True)
                mm.then_inc(var_ready, 1)

            def conv1(mi, j):
                k = mi * NCH + j
                pe.wait_ge(h_done, ONE + k + 1)
                pe.wait_ge(pad_done, ONE + k)
                for b in range(2):
                    mm = pe.matmul(ps_w[:, b, 0:HALF], w1[:, :], h[:, b * HALF:(b + 1) * HALF], start=True, stop=True)
                mm.then_inc(conv1_ready, 1)

            def conv2(mi, j):
                k = mi * NCH + j
                pe.wait_ge(apre_done, ONE + k + 1)
                for b in range(2):
                    mm = pe.matmul(ps_w[:, b, 0:HALF], w2[:, :], h[:, b * HALF:(b + 1) * HALF], start=True, stop=True)
                mm.then_inc(conv2_ready, 1)

            def back(mi, j, parity):
                k = mi * NCH + j
                pe.wait_ge(pad_done, ONE + NCH * (mi + 1))
                pe.wait_ge(taps_taken, ONE + k)
                for tap in range(PE_TAPS):
                    for b in range(2):
                        mm = pe.matmul(image(ps_d)[:, b], diag[:, tap, :], window(pad[parity], j, tap)[:, b],
                                       start=(tap == 0), stop=(tap == PE_TAPS - 1))
                mm.then_inc(taps_ready, 1)

            def project(mi, j, normed):
                k = mi * NCH + j
                if normed is not None:
                    pe.wait_ge(log_done, ONE + normed + 1)
                pe.wait_ge(zrow_done, ONE + mi + 1)
                pe.wait_ge(zcol_done, ONE + mi + 1)
                pe.wait_ge(proj_copied, ONE + 2 * k)
                for o, src in enumerate((zcol, zrow)):
                    for b in range(2):
                        lo = j * CH + b * HALF
                        mm = pe.matmul(ps_p[64 * o:64 * (o + 1), b, 0:HALF], wx[:, o, :], src[:, lo:lo + HALF], start=True, stop=True)
                mm.then_inc(proj_ready, 1)

            def slot(mf, mb, mp, mq, parity, pair):
                for j in range(NCH):
                    conv, prod = lagging(mf, mb, parity, j), projected(mp, mq, parity, j)
                    if mf is not None:
                        front(mf, j, parity)
                    if conv:
                        conv1(*conv[:2])
                    if mf is not None:
                        variance(mf, j, mp, mq)
                    if conv:
                        conv2(*conv[:2])
                    if mb is not None:
                        back(mb, j, 1 - parity)
                    if prod:
                        project(*prod[:2], None if mf is None else mf * NCH + j)

            run(pe, prepare, slot)

        @nc_block.scalar
        def _(act):
            def prepare(q):
                act.wait_ge(prep_done, ONE + q + 1)
                act.wait_ge(a_done, ONE + q * imgs)

            def square(mi, j):
                k = mi * NCH + j
                act.wait_ge(xc_ready, ONE + k + 1)
                act.wait_ge(var_ready, ONE + k)
                act.activation(sq[:, :].rearrange("p (b f) -> p b f", b=2), halves(ps_x), ACT.Square).then_inc(sq_ready, 1)

            def norm(mi, j):
                k = mi * NCH + j
                act.wait_ge(var_ready, ONE + k + 1)
                act.activation(logv[:, :].rearrange("p (b f) -> p b f", b=2), halves(ps_p[0:C]), ACT.Ln, bias=eps[:, 0:1]).then_inc(log_done, 1)
                act.wait_ge(log_done, ONE + k + 1)
                act.wait_ge(h_done, ONE + k)
                act.activation(rstd[:, :], logv[:, :], ACT.Exp, scale=-0.5).then_inc(rstd_ready, 1)

            def first_out(mi, j, parity, before):
                k = mi * NCH + j
                act.wait_ge(conv1_ready, ONE + k + 1)
                if j == 0 and before is not None:
                    act.wait_ge(a_done, ONE + before + 1)
                act.activation(apre[parity][:, rows(j)].rearrange("p (b f) -> p b f", b=2), halves(ps_w), ACT.Identity,
                               bias=bias[:, 0:1]).then_inc(apre_done, 1)

            def second_out(mi, j, parity):
                k = mi * NCH + j
                act.wait_ge(conv2_ready, ONE + k + 1)
                out = pad[parity][:, 1 + j * CROWS:1 + (j + 1) * CROWS, 1:1 + HQ].rearrange("p (b r) w -> p b r w", b=2)
                act.activation(out, image(ps_w), ACT.Identity, bias=bias[:, 1:2]).then_inc(pad_done, 1)

            def project(mi, j, parity, before):
                k = mi * NCH + j
                act.wait_ge(proj_ready, ONE + k + 1)
                if j == 0:
                    act.wait_ge(parts_out[parity], ONE + 16 * 28 * before)
                for dst in (proj, parts):
                    dst = dst[parity] if dst is proj else dst[parity][0]
                    act.activation(dst[:, rows(j)].rearrange("p (b f) -> p b f", b=2), halves(ps_p), ACT.Copy).then_inc(proj_copied, 1)

            def silus(mi, parity):
                act.wait_ge(zpre_done, ONE + NCH * (mi + 1))
                act.wait_ge(apre_done, ONE + NCH * (mi + 1))
                act.wait_ge(proj_ready, ONE + NCH * mi)
                act.wait_ge(zrow_out, ONE + 16 * mi)
                act.wait_ge(a_out, ONE + 16 * mi)
                act.activation(zrow[:, :], zpre[parity][:, :], ACT.Silu, bias=cur[:, 4:5]).then_inc(zrow_done, 1)
                act.activation(a[:, :], apre[parity][:, :], ACT.Silu).then_inc(a_done, 1)

            def slot(mf, mb, mp, mq, parity, pair):
                for j in range(NCH):
                    conv, prod = lagging(mf, mb, parity, j), projected(mp, mq, parity, j)
                    if mf is not None:
                        square(mf, j)
                    if conv:
                        first_out(*conv, mp)
                    if mf is not None:
                        norm(mf, j)
                    if conv:
                        second_out(*conv)
                    if prod:
                        project(*prod, pair)
                    if j == 0 and mp is not None:
                        silus(mp, parity)
                        act.preload_act_table_set(LN_EXP)

            act.preload_act_table_set(LN_EXP)
            act.wait_ge(pads_zeroed, ONE + 3)
            run(act, prepare, slot)

        @nc_block.vector
        def _(dve):
            def prepare(q):
                dve.wait_ge(proj_ready, ONE + q * (imgs * NCH))
                dve.wait_ge(zrow_done, ONE + q * imgs)
                dve.wait_ge(zcol_done, ONE + q * imgs)
                dve.tensor_copy(cur[:, :], vec[:, ds(q, 1), :].rearrange("p a v -> p (a v)"))
                dve.tensor_copy(w1raw[:, :], w1all[:, ds(q, 1), :].rearrange("p a v -> p (a v)"))
                dve.tensor_copy(w2raw[:, :], w2all[:, ds(q, 1), :].rearrange("p a v -> p (a v)"))
                dve.tensor_copy(wx[:, :, :], wxall[:, ds(q, 1), :, :].rearrange("p a o v -> p (a o) v"))
                dve.tensor_copy(dw[:, :], dwall[:, ds(q, 1), :].rearrange("p a v -> p (a v)")).then_inc(prep_raw, 1)
                dve.wait_ge(prep_raw, ONE + q + 1)
                dve.tensor_scalar(w1[:, :], w1raw[:, :], cur[:, 0:1], None, ALU.mult)
                dve.tensor_scalar(w2[:, :], w2raw[:, :], cur[:, 0:1], None, ALU.mult)
                for tap in range(PE_TAPS):
                    dve.tensor_scalar(diag[:, tap, :], ident[:, :], dw[:, tap:tap + 1], None, ALU.mult)
                dve.wait_ge(prep_bias, ONE + q + 1)
                dve.tensor_tensor(bias[:, 0:1], ps_w[:, 0, 0:1], cur[:, 2:3], ALU.add)
                dve.tensor_tensor(bias[:, 1:2], ps_w[:, 1, 0:1], cur[:, 3:4], ALU.add).then_inc(prep_done, 1)
                dve.wait_ge(prep_done, ONE + q + 1)

            def front(mi, j, parity):
                k = mi * NCH + j
                dve.wait_ge(rstd_ready, ONE + k + 1)
                dve.wait_ge(conv2_ready, ONE + k)
                dve.tensor_tensor(h[:, :].rearrange("p (b f) -> p b f", b=2), halves(ps_x),
                                  rstd[:, :].rearrange("p (b f) -> p b f", b=2), ALU.mult).then_inc(h_done, 1)

            def back(mi, j, parity, before, taps):
                k = mi * NCH + j
                for t in taps:
                    tap = PE_TAPS + t
                    out = zpre[parity][:, rows(j)].rearrange("p (b r w) -> p b r w", b=2, w=HQ)
                    if t == 0:
                        dve.wait_ge(taps_ready, ONE + k + 1)
                        if j == 0 and before is not None:
                            dve.wait_ge(zrow_done, ONE + before + 1)
                    elif t == 1:
                        dve.wait_ge(taps_taken, ONE + k + 1)
                    else:
                        dve.wait_ge(dve_tap, ONE + k * (DVE_TAPS - 2) + (t - 1))
                    ins = dve.scalar_tensor_tensor(out=out, in0=window(pad[parity], j, tap), scalar=dw[:, tap:tap + 1],
                                                   in1=image(ps_d) if t == 0 else out, op0=ALU.mult, op1=ALU.add)
                    ins.then_inc(taps_taken if t == 0 else zpre_done if t == DVE_TAPS - 1 else dve_tap, 1)

            def project(mi, j, parity, before):
                k = mi * NCH + j
                dve.wait_ge(proj_copied, ONE + 2 * (k + 1))
                dve.wait_ge(parts_done, ONE + k)
                if j == 0:
                    dve.wait_ge(parts_out[parity], ONE + 16 * 28 * before)
                dve.tensor_tensor(rest[:, :], proj[parity][:, rows(j)], parts[parity][0][:, rows(j)], ALU.subtract).then_inc(rest_done, 1)
                dve.wait_ge(rest_done, ONE + k + 1)
                dve.tensor_copy(parts[parity][1][:, rows(j)], rest[:, :]).then_inc(mid_done, 1)

            def transpose(mi):
                dve.wait_ge(zrow_done, ONE + mi + 1)
                dve.wait_ge(zcol_out, ONE + 16 * mi)
                dve.tensor_copy(zcol[:, :].rearrange("p (w h) -> p w h", w=HQ),
                                zrow[:, :].rearrange("p (h w) -> p w h", w=HQ)).then_inc(zcol_done, 1)

            def slot(mf, mb, mp, mq, parity, pair):
                for j in range(NCH):
                    prod = projected(mp, mq, parity, j)
                    if mf is not None:
                        front(mf, j, parity)
                    if mb is not None:
                        back(mb, j, 1 - parity, mq, range(0, 4))
                    if prod:
                        project(*prod, pair)
                    if j == 0 and mp is not None:
                        transpose(mp)
                    if mb is not None:
                        back(mb, j, 1 - parity, mq, range(4, DVE_TAPS))

            for i in range(2):
                dve.memset(pad[i][:, :, :], 0.0).then_inc(pads_zeroed, 1)
            dve.memset(eps[:, :], LN_EPS).then_inc(pads_zeroed, 1)
            dve.wait_ge(w_in, ONE + 16 * 8)
            run(dve, prepare, slot)

        @nc_block.gpsimd
        def _(pool):
            def project(mi, j, parity):
                k = mi * NCH + j
                pool.wait_ge(mid_done, ONE + k + 1)
                pool.tensor_tensor(parts[parity][2][:, rows(j)], rest[:, :], parts[parity][1][:, rows(j)], ALU.subtract).then_inc(parts_done, 1)

            def slot(mf, mb, mp, mq, parity, pair):
                for j in range(NCH):
                    prod = projected(mp, mq, parity, j)
                    if j == 1 and mp is not None:
                        pool.wait_ge(parts_out[parity], ONE + 16 * 28 * pair)
                    if prod:
                        project(*prod)

            run(pool, nothing, slot)

def scan_phase(nc, d):
    U = d["z"].shape[1] // 128
    UNITS = 4 * NCH * N
    SEG = NCH * N
    SLOTS = 4 * NCH * (N + 1)
    CREDIT = 8
    LAG = 4
    AHEAD = 2
    RA, RC, RH = 3, 6, 6
    DELTA = 2 + AHEAD

    with ExitStack() as ctx:
        m = Memory(nc, ctx, "scan")
        z = [m.sbuf(f"z{o}", [128, L]) for o in range(2)]
        y = [m.sbuf(f"y{o}", [128, L]) for o in range(2)]
        delta = [m.sbuf(f"delta{r}", [128, L]) for r in range(2)]
        du = [m.sbuf(f"du{r}", [128, L]) for r in range(2)]
        bparts = [m.sbuf(f"bparts{r}", [96, L], BF16) for r in range(2)]
        cparts = [m.sbuf(f"cparts{r}", [96, L], BF16) for r in range(2)]
        dts = [m.sbuf(f"dts{r}", [IMGS * R, L]) for r in range(2)]
        select = [m.sbuf(f"select{o}", [96, N, 128], BF16) for o in range(2)]
        wdt = [m.sbuf(f"wdt{o}", [IMGS * R, 2, 128]) for o in range(2)]
        prm = [m.sbuf(f"prm{o}", [128, 2 * N + 4]) for o in range(2)]
        negA = [m.sbuf(f"negA{o}", [128, 2 * N]) for o in range(2)]
        dsum = [m.sbuf(f"dsum{o}", [128, 1]) for o in range(2)]
        ident = m.sbuf("ident", [128, 128])
        dA = m.sbuf("dA", [128, RA, CH])
        csb = m.sbuf("csb", [128, RC, CH])
        hc = m.sbuf("hc", [128, RH, CH])
        h = m.sbuf("h", [128, N, CH])
        relu = m.sbuf("relu", [128, CH])
        soft = m.sbuf("soft", [128, CH])
        tiny = m.sbuf("tiny", [128, 4])
        ps_b = m.psum("ps_b", [128, 2, 2 * BANK])
        ps_c = m.psum("ps_c", [128, 2 * BANK])
        ps_y = m.psum("ps_y", [128, 2 * BANK])

        const_in = m.sem("const_in")
        passed = m.sem("passed")
        z_in = [m.sem(f"z_in{o}") for o in range(2)]
        prm_in = [m.sem(f"prm_in{o}") for o in range(2)]
        dts_in = [m.sem(f"dts_in{r}") for r in range(2)]
        bc_in = [m.sem(f"bc_in{r}") for r in range(2)]
        y_out = [m.sem(f"y_out{o}") for o in range(2)]
        negA_step = m.sem("negA_step")
        negA_ready = m.sem("negA_ready")
        dsum_ready = m.sem("dsum_ready")
        b_ready = m.sem("b_ready")
        c_ready = m.sem("c_ready")
        c_evac = m.sem("c_evac")
        dA_ready = m.sem("dA_ready")
        dbu_ready = m.sem("dbu_ready")
        scan_done = m.sem("scan_done")
        hc_done = m.sem("hc_done")
        y_summed = m.sem("y_summed")
        y_evac = m.sem("y_evac")
        abs_done = m.sem("abs_done")
        exp_done = m.sem("exp_done")
        soft_ready = m.sem("soft_ready")
        delta_done = m.sem("delta_done")
        du_done = m.sem("du_done")

        order = [list(range(NCH)), list(range(NCH))[::-1]]

        def cols(i, r):
            c = order[r][i]
            return slice(c * CH, (c + 1) * CH)

        def slot(u, s, i, pos):
            return u * SLOTS + (NCH + (s * NCH + i) * (N + 1) + pos)

        def unit(u, s, i, n):
            return u * UNITS + (s * SEG + i * N + n)

        def pos(n):
            return n if n < DELTA else n + 1

        def pieces():
            return [(0, BANK), (BANK, CH)]

        def ring(depth, s, i, n):
            return (s * SEG + i * N + n) % depth

        def after(u, k, lead):
            return (u if k + lead < UNITS else u + 1,) + steps[(k + lead) % UNITS]

        steps = [(s, i, n) for s in range(4) for i in range(NCH) for n in range(N)]

        m.start()
        nc_block = ctx.enter_context(nc.Block())

        @nc_block.sync
        def _(sp):
            def load_z(o, u, t):
                sp.dma_start(z[o][:, :], d["z"][o, ds(u * 128, 128), :]).then_inc(z_in[o], 16)
                sp.dma_start(prm[o][:, :], d["prm"][ds(u, 1), o, :, :].rearrange("a p c -> (a p) c")).then_inc(prm_in[o], 16)
                sp.dma_start(wdt[o][:, :, :], d["wdt"][ds(u, 1), o, :, :, :].rearrange("a k r p -> (a k) r p")).then_inc(prm_in[o], 16)
                sp.dma_start(select[o][:, :, :], d["select"][ds(t, 1), :, :, :].rearrange("a k n p -> (a k) n p")).then_inc(prm_in[o], 16)

            def load_dts(o, r, st):
                sp.dma_start(dts[r][:, :], d["dts"][ds(st, 1), o, r, :, :].rearrange("a k l -> (a k) l")).then_inc(dts_in[r], 16)

            def load_bc(o, r, st):
                for k, t in enumerate((bparts[r], cparts[r])):
                    sp.dma_start(t[:, :], d["bc"][ds(st, 1), o, k, r, :, :, :].rearrange("a i j l -> (a i j) l")).then_inc(bc_in[r], 16)

            sp.dma_start(ident[:, :], d["ident"][:, :]).then_inc(const_in, 16)
            load_dts(0, 0, 0)
            load_z(0, 0, 0)
            load_bc(0, 0, 0)
            load_dts(0, 1, 0)

            def write_y(o, u):
                sp_wait(sp, passed, (y_evac, ONE + CREDIT + u * 4 * NCH + (o + 1) * 2 * NCH))
                sp.dma_start(d["y"][o, ds(u * 128, 128), :], y[o][:, :]).then_inc(y_out[o], 16)

            def body(u, first=False):
                keep = (lambda value: value) if first else sp.snap
                nxt = keep((u + 1) % U)
                tile, next_tile = keep(u % TILES), keep(nxt % TILES)
                group, next_group = keep(u // TILES), keep(nxt // TILES)
                for s in range(4):
                    o, r = divmod(s, 2)
                    sp_wait(sp, passed, (b_ready, ONE + unit(u, s, 0, 0)), (c_ready, ONE + slot(u, s, 0, 0)))
                    load_dts((o + 1) % 2, r, group if s < 2 else next_group)
                    if s == 0:
                        load_z(1, u, tile)
                    if s == 2:
                        load_z(0, nxt, next_tile)
                    so, sr = divmod((s + 1) % 4, 2)
                    load_bc(so, sr, group if s < 3 else next_group)
                    if s == 0 and not first:
                        write_y(1, u - 1)
                    if s == 2:
                        write_y(0, u)

            body(0, first=True)
            with sp.Fori(1, U) as u:
                body(u)
            write_y(1, U - 1)
            for o in range(2):
                sp_wait(sp, passed, (y_out[o], ONE + 16 * U))
            sp_wait(sp, passed, (z_in[0], ONE + 16 * (U + 1)), (z_in[1], ONE + 16 * U), (prm_in[0], ONE + 48 * (U + 1)), (prm_in[1], ONE + 48 * U))
            for r in range(2):
                sp_wait(sp, passed, (dts_in[r], ONE + 16 * (2 * U + 1)))
            sp_wait(sp, passed, (bc_in[0], ONE + 32 * (2 * U + 1)), (bc_in[1], ONE + 32 * 2 * U))

        @nc_block.tensor
        def _(pe):
            def delta_product(u, s, i, use):
                o, r = divmod(s, 2)
                pe.wait_ge(dts_in[r], ONE + 16 * (2 * u + o + 1))
                pe.wait_ge(prm_in[o], ONE + 48 * (u + 1))
                pe.wait_ge(c_evac, ONE + use)
                a = cols(i, r).start
                for lo, hi in pieces():
                    mm = pe.matmul(ps_c[:, lo:hi], wdt[o][:, r, :], dts[r][:, a + lo:a + hi], start=True, stop=True)
                mm.then_inc(c_ready, 1)

            def spread_b(u, s, i, n):
                o, r = divmod(s, 2)
                a = cols(i, r).start
                if i == 0 and n == 0:
                    pe.wait_ge(bc_in[r], ONE + 32 * (2 * u + o + 1))
                k = unit(u, s, i, n)
                pe.wait_ge(scan_done, ONE + CREDIT + k - 1)
                for lo, hi in pieces():
                    mm = pe.matmul(ps_b[:, n % 2, lo:hi], select[o][:, n, :], bparts[r][:, a + lo:a + hi], start=True, stop=True)
                mm.then_inc(b_ready, 1)

            def spread_c(u, s, i, n):
                o, r = divmod(s, 2)
                a = cols(i, r).start
                if i == 0 and n == 0:
                    pe.wait_ge(bc_in[r], ONE + 32 * (2 * u + o + 1))
                    pe.wait_ge(prm_in[o], ONE + 48 * (u + 1))
                pe.wait_ge(c_evac, ONE + slot(u, s, i, pos(n)))
                for lo, hi in pieces():
                    mm = pe.matmul(ps_c[:, lo:hi], select[o][:, n, :], cparts[r][:, a + lo:a + hi], start=True, stop=True)
                mm.then_inc(c_ready, 1)

            def sum_states(u, s, i, n):
                if n == 0:
                    pe.wait_ge(y_evac, ONE + CREDIT + u * 4 * NCH + s * NCH + i)
                pe.wait_ge(hc_done, ONE + CREDIT + unit(u, s, i, n) + 1)
                for lo, hi in pieces():
                    mm = pe.matmul(ps_y[:, lo:hi], ident[:, :], hc[:, ring(RH, s, i, n), lo:hi], start=(n == 0), stop=(n == N - 1))
                mm.then_inc(y_summed, 1)

            pe.wait_ge(const_in, ONE + 16)
            for i in range(NCH):
                delta_product(0, 0, i, i)
            for k in range(AHEAD):
                spread_c(0, *steps[k])

            def body(u, first=False):
                for k, (s, i, n) in enumerate(steps):
                    spread_b(u, s, i, n)
                    if n < 2:
                        spread_c(*after(u, k, AHEAD))
                    if k >= LAG:
                        sum_states(u, *steps[k - LAG])
                    elif not first:
                        sum_states(u - 1, *steps[k - LAG])
                    if n == 1:
                        delta_product(*after(u, k, SEG)[:3], slot(u, s, i, DELTA))
                    if n >= 2:
                        spread_c(*after(u, k, AHEAD))

            body(0, first=True)
            with pe.Fori(1, U) as u:
                body(u)
            for st in steps[-LAG:]:
                sum_states(U - 1, *st)

        @nc_block.scalar
        def _(act):
            def neg_a(u, o):
                act.wait_ge(prm_in[o], ONE + 48 * (u + 1))
                act.activation(negA[o][:, :], prm[o][:, 0:2 * N], ACT.Exp).then_inc(negA_step, 1)
                act.wait_ge(negA_step, ONE + 2 * u + (o + 1))
                act.activation(negA[o][:, :], negA[o][:, :], ACT.Copy, scale=-1.0).then_inc(negA_ready, 1)

            def softplus_terms(u, s, i, use):
                o, r = divmod(s, 2)
                j = u * 4 * NCH + (s * NCH + i)
                bias = prm[o][:, 2 * N + 2 + r:2 * N + 3 + r]
                act.wait_ge(c_ready, ONE + use + 1)
                act.wait_ge(delta_done, ONE + j)
                act.activation(relu[:, :], ps_c[:, 0:CH], ACT.Relu, bias=bias)
                act.activation(soft[:, :], ps_c[:, 0:CH], ACT.Abs, bias=bias).then_inc(c_evac, 1)

            def softplus_exp(u, s, i, use):
                act.wait_ge(c_evac, ONE + use + 1)
                act.activation(soft[:, :], soft[:, :], ACT.Exp, scale=-1.0).then_inc(exp_done, 1)

            def softplus_log(u, s, i):
                j = u * 4 * NCH + (s * NCH + i)
                act.wait_ge(exp_done, ONE + j + 1)
                act.activation(soft[:, :], soft[:, :], ACT.Ln, bias=1.0).then_inc(soft_ready, 1)

            def decay(u, s, i, n):
                o, r = divmod(s, 2)
                k = unit(u, s, i, n)
                if n == 0:
                    act.wait_ge(delta_done, ONE + u * 4 * NCH + (s * NCH + i) + 1)
                    if i == 0 and r == 0:
                        act.wait_ge(negA_ready, ONE + 2 * u + (o + 1))
                act.wait_ge(scan_done, ONE + CREDIT + k - (RA - 1))
                act.activation(dA[:, ring(RA, s, i, n), :], delta[r][:, cols(i, r)], ACT.Exp,
                               scale=negA[o][:, r * N + n:r * N + n + 1]).then_inc(dA_ready, 1)

            def evacuate_c(u, s, i, n):
                act.wait_ge(c_ready, ONE + slot(u, s, i, pos(n)) + 1)
                act.wait_ge(hc_done, ONE + CREDIT + unit(u, s, i, n) - (RC - 1))
                act.activation(csb[:, ring(RC, s, i, n), :], ps_c[:, 0:CH], ACT.Copy).then_inc(c_evac, 1)

            act.preload_act_table_set(LN_EXP)
            neg_a(0, 0)
            for i in range(NCH):
                softplus_terms(0, 0, i, i)
                softplus_exp(0, 0, i, i)
                softplus_log(0, 0, i)
            for k in range(AHEAD):
                evacuate_c(0, *steps[k])
            decay(0, 0, 0, 0)
            with act.Fori(0, U) as u:
                for k, (s, i, n) in enumerate(steps):
                    decay(*after(u, k, 1))
                    evacuate_c(*after(u, k, AHEAD))
                    coming = after(u, k, SEG)[:3]
                    if n == 1:
                        softplus_terms(*coming, slot(u, s, i, DELTA))
                    if n == 2:
                        softplus_exp(*coming, slot(u, s, i, DELTA))
                    if n == 3:
                        softplus_log(*coming)
                    if (i, n) == (1, 6) and s == 0:
                        neg_a(u, 1)
                    if (i, n) == (1, 6) and s == 2:
                        neg_a(u + 1, 0)

        @nc_block.vector
        def _(dve):
            def add_d(u, o):
                dve.wait_ge(prm_in[o], ONE + 48 * (u + 1))
                dve.tensor_tensor(dsum[o][:, :], prm[o][:, 2 * N:2 * N + 1], prm[o][:, 2 * N + 1:2 * N + 2],
                                  ALU.add).then_inc(dsum_ready, 1)

            def evacuate(u, s, i):
                o, r = divmod(s, 2)
                j = u * 4 * NCH + (s * NCH + i)
                dve.wait_ge(y_summed, ONE + CREDIT + unit(u, s, i, N - 1) + 1)
                part = y[o][:, cols(i, r)]
                if r == 0:
                    dve.wait_ge(dsum_ready, ONE + 2 * u + (o + 1))
                    dve.wait_ge(y_out[o], ONE + 16 * u)
                    dve.scalar_tensor_tensor(out=part, in0=z[o][:, cols(i, r)], scalar=dsum[o][:, 0:1],
                                             in1=ps_y[:, 0:CH], op0=ALU.mult, op1=ALU.add).then_inc(y_evac, 1)
                else:
                    dve.tensor_tensor(part, part, ps_y[:, 0:CH], ALU.add).then_inc(y_evac, 1)

            dve.memset(tiny[:, 0:1], 0.0).then_inc(scan_done, CREDIT)
            dve.memset(tiny[:, 1:2], 0.0).then_inc(y_evac, CREDIT)
            dve.memset(tiny[:, 3:4], 0.0).then_inc(y_summed, CREDIT)
            add_d(0, 0)

            def body(u, first_tile=False):
                for s, i, n in steps:
                    o, r = divmod(s, 2)
                    k = unit(u, s, i, n)
                    j = u * 4 * NCH + (s * NCH + i)
                    if n == 0:
                        dve.wait_ge(du_done, ONE + j + 1)
                    dve.wait_ge(b_ready, ONE + k + 1)
                    dbu = ps_b[:, n % 2, 0:CH]
                    dve.tensor_tensor(dbu, du[r][:, cols(i, r)], dbu, ALU.mult).then_inc(dbu_ready, 1)
                    if n == LAG - 1:
                        if (s, i) != (0, 0):
                            evacuate(u, *divmod(s * NCH + i - 1, NCH))
                        elif not first_tile:
                            evacuate(u - 1, 3, NCH - 1)
                    dve.wait_ge(dbu_ready, ONE + k + 1)
                    dve.wait_ge(dA_ready, ONE + k + 1)
                    dve.wait_ge(hc_done, ONE + CREDIT + k - 7)
                    dec, out = dA[:, ring(RA, s, i, n), :], h[:, n, :]
                    if r == 0:
                        first = h[:, n, CH - 1:CH]
                    else:
                        dec, out, dbu = dec[:, ::-1], out[:, ::-1], dbu[:, ::-1]
                        first = h[:, n, 0:1]
                    dve.tensor_tensor_scan(out, dec, dbu, 0.0 if i == 0 else first, ALU.mult, ALU.add).then_inc(scan_done, 1)
                    if (i, n) == (NCH - 1, N - 1):
                        if s == 0:
                            add_d(u, 1)
                        if s == 2:
                            add_d(u + 1, 0)

            body(0, first_tile=True)
            with dve.Fori(1, U) as u:
                body(u)
            evacuate(U - 1, 3, NCH - 1)

        @nc_block.gpsimd
        def _(pool):
            def finish_delta(u, s, i):
                o, r = divmod(s, 2)
                j = u * 4 * NCH + (s * NCH + i)
                pool.wait_ge(soft_ready, ONE + j + 1)
                part = delta[r][:, cols(i, r)]
                pool.tensor_tensor(part, relu[:, :], soft[:, :], ALU.add).then_inc(delta_done, 1)

            def scale_input(u, s, i):
                o, r = divmod(s, 2)
                j = u * 4 * NCH + (s * NCH + i)
                part = delta[r][:, cols(i, r)]
                pool.wait_ge(delta_done, ONE + j + 1)
                pool.wait_ge(z_in[o], ONE + 16 * (u + 1))
                pool.tensor_tensor(du[r][:, cols(i, r)], part, z[o][:, cols(i, r)], ALU.mult).then_inc(du_done, 1)

            pool.memset(tiny[:, 2:3], 0.0).then_inc(hc_done, CREDIT)
            for i in range(NCH):
                finish_delta(0, 0, i)
                scale_input(0, 0, i)
            with pool.Fori(0, U) as u:
                for s, i, n in steps:
                    k = unit(u, s, i, n)
                    pool.wait_ge(c_evac, ONE + slot(u, s, i, pos(n)) + 1)
                    pool.wait_ge(scan_done, ONE + CREDIT + k + 1)
                    pool.wait_ge(y_summed, ONE + CREDIT + k - (RH - 1))
                    pool.tensor_tensor(hc[:, ring(RH, s, i, n), :], h[:, n, :], csb[:, ring(RC, s, i, n), :],
                                       ALU.mult).then_inc(hc_done, 1)
                    ns, nu = ((s + 1) % 4, u if s < 3 else u + 1)
                    if n == 4:
                        finish_delta(nu, ns, i)
                    if n == 6:
                        scale_input(nu, ns, i)

def gate_phase(nc, d):
    imgs = d["x"].shape[1]
    with ExitStack() as ctx:
        m = Memory(nc, ctx, "gate")
        center = m.sbuf("center", [C, C])
        mean = m.sbuf("mean", [C, C])
        eps = m.sbuf("eps", [C, 1])
        vec = m.sbuf("vec", [C, NQ, 5])
        ca1 = m.sbuf("ca1", [C, NQ, CR])
        ca2 = m.sbuf("ca2", [CR, NQ, C])
        cab1 = m.sbuf("cab1", [CR, NQ])
        cur = m.sbuf("cur", [C, 5])
        cg = m.sbuf("cg", [C, C])
        cb = m.sbuf("cb", [C, 1])
        wa1 = m.sbuf("wa1", [C, CR])
        wa2 = m.sbuf("wa2", [CR, C])
        ba1 = m.sbuf("ba1", [CR, 1])
        ycol = [m.sbuf(f"ycol{i}", [C, L]) for i in range(2)]
        yrow = [m.sbuf(f"yrow{i}", [C, L]) for i in range(2)]
        a = [m.sbuf(f"a{i}", [C, L]) for i in range(2)]
        x = [m.sbuf(f"x{i}", [C, L]) for i in range(2)]
        y = [m.sbuf(f"y{i}", [C, L]) for i in range(2)]
        ysum = m.sbuf("ysum", [C, 2, CH])
        sq = m.sbuf("sq", [C, CH])
        sq2 = m.sbuf("sq2", [C, CH])
        logv = m.sbuf("logv", [C, CH])
        logv2 = m.sbuf("logv2", [C, CH])
        rstd = m.sbuf("rstd", [C, CH])
        rstd2 = m.sbuf("rstd2", [C, CH])
        s1 = m.sbuf("s1", [C, CH])
        z2 = m.sbuf("z2", [C, CH])
        z3 = m.sbuf("z3", [C, CH])
        total = [m.sbuf(f"total{i}", [C, NCH]) for i in range(2)]
        hid = m.sbuf("hid", [CR, 5])
        att = m.sbuf("att", [C, 4])
        ps_x = [m.psum(f"ps_x{i}", [C, 2, BANK]) for i in range(2)]
        ps_x2 = m.psum("ps_x2", [C, 2, BANK])
        ps_v = m.psum("ps_v", [C, 2, BANK])
        ps_t = ps_v[:, 1, HALF:HALF + 1]

        w_in = m.sem("w_in")
        passed = m.sem("passed")
        y_in = [m.sem(f"y_in{i}") for i in range(2)]
        a_in = [m.sem(f"a_in{i}") for i in range(2)]
        x_in = [m.sem(f"x_in{i}") for i in range(2)]
        x_out = [m.sem(f"x_out{i}") for i in range(2)]
        eps_set = m.sem("eps_set")
        prep_raw = m.sem("prep_raw")
        prep_cb = m.sem("prep_cb")
        prep_done = m.sem("prep_done")
        ysum_done = m.sem("ysum_done")
        x_ready = m.sem("x_ready")
        x2_ready = m.sem("x2_ready")
        sq_ready = m.sem("sq_ready")
        sq2_ready = m.sem("sq2_ready")
        var_ready = m.sem("var_ready")
        var2_ready = m.sem("var2_ready")
        log_done = m.sem("log_done")
        log2_done = m.sem("log2_done")
        rstd_ready = m.sem("rstd_ready")
        rstd2_ready = m.sem("rstd2_ready")
        s1_done = m.sem("s1_done")
        z2_done = m.sem("z2_done")
        z3_done = m.sem("z3_done")
        y_done = m.sem("y_done")
        hid_ready = m.sem("hid_ready")
        hid_exp = m.sem("hid_exp")
        hid_step = m.sem("hid_step")
        hid_done = m.sem("hid_done")
        att_ready = m.sem("att_ready")
        att_exp = m.sem("att_exp")
        att_step = m.sem("att_step")
        x1_done = m.sem("x1_done")

        def rows(j):
            return slice(j * CH, (j + 1) * CH)

        def two(ap):
            return ap.rearrange("p (b f) -> p b f", b=2)

        def run(eng, prepare, slot):
            with eng.Fori(0, NQ) as q:
                base = q * imgs
                prepare(q, base)
                slot(base, None, base + 1, 0)
                with eng.Fori(0, (imgs - 2) // 2) as i:
                    slot(base + i * 2 + 1, base + i * 2, base + i * 2 + 2, 1)
                    slot(base + i * 2 + 2, base + i * 2 + 1, base + i * 2 + 3, 0)
                slot(base + (imgs - 1), base + (imgs - 2), None, 1)
                slot(None, base + (imgs - 1), None, 0)

        def j_ring(parity, j):
            return (parity * NCH + j) % 2

        def ahead(mi, nxt, parity, j):
            if j < NCH - 1:
                return None if mi is None else (mi, j + 1, parity)
            return None if nxt is None else (nxt, 0, 1 - parity)

        def second(mi, prev, j):
            if j == 0:
                return None if prev is None else prev * NCH + (NCH - 1)
            return None if mi is None else mi * NCH + (j - 1)

        m.start()
        nc_block = ctx.enter_context(nc.Block())

        @nc_block.sync
        def _(sp):
            for tile, name in ((center, "center"), (mean, "mean"), (vec, "gate_vec"), (ca1, "ca_w1"), (ca2, "ca_w2"), (cab1, "ca_b1")):
                sp.dma_start(tile[tuple([slice(None)] * len(tile.shape))], d[name]).then_inc(w_in, 16)

            def load_y(mi, parity):
                for t, o in ((ycol, 0), (yrow, 1)):
                    sp.dma_start(t[parity][:, :], d["y"][o, ds(mi * C, C), :]).then_inc(y_in[parity], 16)

            def load_a(mi, parity):
                sp.dma_start(a[parity][:, :], d["a"][ds(mi * C, C), :]).then_inc(a_in[parity], 16)

            def slot(mi, prev, nxt, parity):
                if mi is not None:
                    half, after = sp.snap(mi // 2), sp.snap((mi + 1) % (NQ * imgs))
                    sp_wait(sp, passed, (ysum_done, ONE + NCH * mi))
                    load_y(after, 1 - parity)
                    sp_wait(sp, passed, (x_out[parity], ONE + 16 * half))
                    sp.dma_start(x[parity][:, :], d["x_flat"][ds(mi * C, C), :]).then_inc(x_in[parity], 16)
                    sp_wait(sp, passed, (y_done, ONE + NCH * mi))
                    load_a(after, 1 - parity)
                if prev is not None:
                    sp_wait(sp, passed, (x1_done, ONE + prev + 1))
                    sp.dma_start(d["x1"][ds(prev * C, C), :], x[1 - parity][:, :]).then_inc(x_out[1 - parity], 16)

            load_y(0, 0)
            load_a(0, 0)
            run(sp, lambda *_: None, slot)
            for i in range(2):
                sp_wait(sp, passed, (x_out[i], ONE + 16 * NQ * imgs // 2))
            sp_wait(sp, passed, (y_in[0], ONE + 32 * (NQ * imgs // 2 + 1)), (a_in[0], ONE + 16 * (NQ * imgs // 2 + 1)))

        @nc_block.gpsimd
        def _(pool):
            def slot(mi, prev, nxt, parity):
                if mi is None:
                    return
                pool.wait_ge(y_in[parity], ONE + 32 * (mi // 2 + 1))
                for j in range(NCH):
                    k = mi * NCH + j
                    if prev is not None or j >= 2:
                        pool.wait_ge(x_ready, ONE + k - 1)
                    else:
                        pool.wait_ge(x_ready, ONE + mi * NCH)
                    col = ycol[parity][:, :].rearrange("p (w h) -> p h w", w=HQ)[:, j * CROWS:(j + 1) * CROWS, :]
                    row = yrow[parity][:, rows(j)].rearrange("p (h w) -> p h w", w=HQ)
                    pool.tensor_tensor(ysum[:, j_ring(parity, j), :].rearrange("p (h w) -> p h w", w=HQ), row, col, ALU.add).then_inc(ysum_done, 1)

            run(pool, lambda *_: None, slot)

        @nc_block.tensor
        def _(pe):
            def prepare(q, base):
                pe.wait_ge(prep_raw, ONE + q + 1)
                pe.matmul(ps_t[:, :], center[:, :], cur[:, 1:2], start=True, stop=True).then_inc(prep_cb, 1)
                pe.wait_ge(prep_done, ONE + q + 1)
                pe.wait_ge(s1_done, ONE + base * NCH)
                centered(base, 0, 0)

            def product(dst, w, src, sem):
                for b in range(2):
                    mm = pe.matmul(dst[:, b, 0:HALF], w[:, :], src[:, b * HALF:(b + 1) * HALF], start=True, stop=True)
                mm.then_inc(sem, 1)

            def centered(mi, j, parity):
                pe.wait_ge(ysum_done, ONE + mi * NCH + (j + 1))
                product(ps_x[j_ring(parity, j)], center, ysum[:, j_ring(parity, j), :], x_ready)

            def slot(mi, prev, nxt, parity):
                for j in range(NCH):
                    to_center = ahead(mi, nxt, parity, j)
                    if to_center:
                        pe.wait_ge(s1_done, ONE + mi * NCH + j)
                        centered(*to_center)
                    if j == 2 and prev is not None:
                        pe.wait_ge(y_done, ONE + NCH * (prev + 1))
                        pe.wait_ge(log2_done, ONE + (NCH * (prev + 1) if mi is None else NCH * mi + 1))
                        for c in range(NCH):
                            mm = pe.matmul(ps_t[0:CR, :], wa1[:, :], total[1 - parity][:, c:c + 1], start=(c == 0), stop=(c == NCH - 1))
                        mm.then_inc(hid_ready, 1)
                        pe.wait_ge(hid_exp, ONE + 2 * prev + 1)
                    if mi is not None:
                        k = mi * NCH + j
                        pe.wait_ge(sq_ready, ONE + k + 1)
                        pe.wait_ge(log2_done, ONE + (k if prev is None and j == 0 else k - 1))
                        product(ps_v, mean, sq, var_ready)
                    p = second(mi, prev, j)
                    if p is not None:
                        pe.wait_ge(s1_done, ONE + p + 1)
                        pe.wait_ge(z2_done, ONE + p)
                        product(ps_x2, cg, s1, x2_ready)
                    if j == 2 and prev is not None:
                        pe.wait_ge(hid_done, ONE + prev + 1)
                        if mi is not None:
                            pe.wait_ge(log_done, ONE + k + 1)
                        pe.matmul(ps_t[:, :], wa2[:, :], hid[:, 4:5], start=True, stop=True).then_inc(att_ready, 1)
                        pe.wait_ge(att_exp, ONE + 2 * prev + 1)
                    if p is not None:
                        pe.wait_ge(sq2_ready, ONE + p + 1)
                        pe.wait_ge(log_done, ONE + (p + 2 if mi is not None else p + 1))
                        product(ps_v, mean, sq2, var2_ready)

            run(pe, prepare, slot)

        @nc_block.scalar
        def _(act):
            def prepare(q, base):
                act.wait_ge(prep_done, ONE + q + 1)
                square(base, 0, 0)

            def square(mi, j, parity):
                k = mi * NCH + j
                act.wait_ge(x_ready, ONE + k + 1)
                act.wait_ge(var_ready, ONE + k)
                act.activation(two(sq[:, :]), halves(ps_x[j_ring(parity, j)]), ACT.Square).then_inc(sq_ready, 1)

            def slot(mi, prev, nxt, parity):
                for j in range(NCH):
                    p = second(mi, prev, j)
                    if j == 2 and prev is not None:
                        act.wait_ge(hid_ready, ONE + prev + 1)
                        act.activation(hid[:, 0:1], ps_t[0:CR, :], ACT.Identity, bias=ba1[:, 0:1], scale=1.0 / L).then_inc(hid_exp, 1)
                        act.wait_ge(hid_exp, ONE + 2 * prev + 1)
                        act.activation(hid[:, 1:2], hid[:, 0:1], ACT.Exp, scale=-1.0).then_inc(hid_exp, 1)
                    if mi is not None:
                        k = mi * NCH + j
                        act.wait_ge(var_ready, ONE + k + 1)
                        act.activation(two(logv[:, :]), halves(ps_v), ACT.Ln, bias=eps[:, 0:1]).then_inc(log_done, 1)
                        act.wait_ge(log_done, ONE + k + 1)
                        act.wait_ge(s1_done, ONE + k)
                        act.activation(rstd[:, :], logv[:, :], ACT.Exp, scale=-0.5).then_inc(rstd_ready, 1)
                    if p is not None:
                        act.wait_ge(x2_ready, ONE + p + 1)
                        act.wait_ge(var2_ready, ONE + p)
                        act.activation(two(sq2[:, :]), halves(ps_x2), ACT.Square, bias=cb[:, 0:1]).then_inc(sq2_ready, 1)
                    if j == 2 and prev is not None:
                        act.wait_ge(att_ready, ONE + prev + 1)
                        act.activation(att[:, 0:1], ps_t[:, :], ACT.Identity, bias=cur[:, 4:5]).then_inc(att_exp, 1)
                        act.wait_ge(att_exp, ONE + 2 * prev + 1)
                        act.activation(att[:, 1:2], att[:, 0:1], ACT.Exp, scale=-1.0).then_inc(att_exp, 1)
                    to_square = ahead(mi, nxt, parity, j)
                    if to_square:
                        square(*to_square)
                    if p is not None:
                        act.wait_ge(var2_ready, ONE + p + 1)
                        act.activation(two(logv2[:, :]), halves(ps_v), ACT.Ln, bias=eps[:, 0:1]).then_inc(log2_done, 1)
                        act.wait_ge(log2_done, ONE + p + 1)
                        act.wait_ge(z2_done, ONE + p)
                        act.activation(rstd2[:, :], logv2[:, :], ACT.Exp, scale=-0.5).then_inc(rstd2_ready, 1)

            act.preload_act_table_set(LN_EXP)
            act.wait_ge(eps_set, ONE + 1)
            run(act, prepare, slot)

        @nc_block.vector
        def _(dve):
            def prepare(q, base):
                dve.wait_ge(x1_done, ONE + base)
                dve.wait_ge(x_ready, ONE + base * NCH)
                for dst, src in ((cur, vec), (wa1, ca1), (wa2, ca2)):
                    dve.tensor_copy(dst[:, :], src[:, ds(q, 1), :].rearrange("p a v -> p (a v)"))
                dve.tensor_copy(ba1[:, :], cab1[:, ds(q, 1)]).then_inc(prep_raw, 1)
                dve.wait_ge(prep_raw, ONE + q + 1)
                dve.tensor_scalar(cg[:, :], center[:, :], cur[:, 0:1], None, ALU.mult)
                dve.wait_ge(prep_cb, ONE + q + 1)
                dve.tensor_copy(cb[:, :], ps_t[:, :]).then_inc(prep_done, 1)

            def slot(mi, prev, nxt, parity):
                for j in range(NCH):
                    p = second(mi, prev, j)
                    if j == 2 and prev is not None:
                        dve.wait_ge(hid_exp, ONE + 2 * (prev + 1))
                        dve.tensor_scalar(hid[:, 2:3], hid[:, 1:2], 1.0, None, ALU.add).then_inc(hid_step, 1)
                        dve.wait_ge(hid_step, ONE + 2 * prev + 1)
                        dve.reciprocal(hid[:, 3:4], hid[:, 2:3]).then_inc(hid_step, 1)
                        dve.wait_ge(hid_step, ONE + 2 * prev + 2)
                        dve.tensor_tensor(hid[:, 4:5], hid[:, 3:4], hid[:, 0:1], ALU.mult).then_inc(hid_done, 1)
                    if mi is not None:
                        k = mi * NCH + j
                        dve.wait_ge(rstd_ready, ONE + k + 1)
                        if p is not None:
                            dve.wait_ge(x2_ready, ONE + p + 1)
                        dve.tensor_tensor(two(s1[:, :]), halves(ps_x[j_ring(parity, j)]), two(rstd[:, :]), ALU.mult).then_inc(s1_done, 1)
                    if p is not None:
                        pj = (j - 1) % NCH
                        par = 1 - parity if j == 0 else parity
                        image = prev if j == 0 else mi
                        dve.wait_ge(rstd2_ready, ONE + p + 1)
                        dve.scalar_tensor_tensor(out=two(z2[:, :]), in0=halves(ps_x2), scalar=cb[:, 0:1], in1=two(rstd2[:, :]),
                                                 op0=ALU.add, op1=ALU.mult).then_inc(z2_done, 1)
                        dve.wait_ge(z2_done, ONE + p + 1)
                        dve.tensor_scalar(z3[:, :], z2[:, :], cur[:, 2:3], cur[:, 3:4], ALU.mult, ALU.add).then_inc(z3_done, 1)
                        dve.wait_ge(z3_done, ONE + p + 1)
                        dve.wait_ge(a_in[par], ONE + 16 * (image // 2 + 1))
                        dve.scalar_tensor_tensor(out=y[par][:, rows(pj)], in0=z3[:, :], scalar=1.0, in1=a[par][:, rows(pj)],
                                                 op0=ALU.mult, op1=ALU.mult, accum_out=total[par][:, pj:pj + 1]).then_inc(y_done, 1)
                    if j == 2 and prev is not None:
                        dve.wait_ge(att_exp, ONE + 2 * (prev + 1))
                        dve.tensor_scalar(att[:, 2:3], att[:, 1:2], 1.0, None, ALU.add).then_inc(att_step, 1)
                        dve.wait_ge(att_step, ONE + 2 * prev + 1)
                        dve.reciprocal(att[:, 3:4], att[:, 2:3]).then_inc(att_step, 1)
                        dve.wait_ge(att_step, ONE + 2 * prev + 2)
                        dve.wait_ge(x_in[1 - parity], ONE + 16 * (prev // 2 + 1))
                        xt = x[1 - parity][:, :]
                        dve.scalar_tensor_tensor(out=xt, in0=y[1 - parity][:, :], scalar=att[:, 3:4], in1=xt,
                                                 op0=ALU.mult, op1=ALU.add).then_inc(x1_done, 1)

            dve.memset(eps[:, :], LN_EPS).then_inc(eps_set, 1)
            dve.wait_ge(w_in, ONE + 16 * 6)
            run(dve, prepare, slot)

def residual_phase(nc, d):
    M = 576
    S = 2 * HQ
    ROWS = 16
    HT = ROWS + 2
    SUBS = 2
    SR = ROWS // SUBS
    SC = SR * S
    BR = SR // 2
    imgs = d["x"].shape[1]
    TAPS = [(dy, dx) for dy in range(3) for dx in range(3)]
    PE_TAPS, POOL_TAPS = [0], [1, 2, 3]
    DVE_TAPS = [t for t in range(9) if t not in PE_TAPS + POOL_TAPS]
    PAIRS = S // ROWS // 2
    JOBS_PAIR = 9
    JOBS_IMG = PAIRS * JOBS_PAIR
    JOBS = 2 * JOBS_IMG
    PIECES = ROWS // BR
    CREDIT = 8

    with ExitStack() as ctx:
        m = Memory(nc, ctx, "res")
        x = [m.sbuf(f"x{i}", [C, NQ, HQ, HQ]) for i in range(2)]
        w1 = m.sbuf("w1", [C, M])
        w3 = m.sbuf("w3", [C, M])
        w3s = m.sbuf("w3s", [128, 5, C])
        wd = m.sbuf("wd", [128, 5, 9])
        bn = m.sbuf("bn", [128, 5, 8])
        bn3 = m.sbuf("bn3", [C, 4])
        sc = m.sbuf("sc", [128, 5, 2])
        bi = m.sbuf("bi", [128, 5, 2])
        sc3 = m.sbuf("sc3", [C, 1])
        bi3 = m.sbuf("bi3", [C, 1])
        eps = m.sbuf("eps", [128, 1])
        ident = m.sbuf("ident", [128, 128])
        diag = m.sbuf("diag", [128, 5, len(PE_TAPS), 128])
        diag3 = m.sbuf("diag3", [C, C])
        zeros = m.sbuf("zeros", [128, S])
        hid = [m.sbuf(f"hid{i}", [128, HT, S + 2]) for i in range(2)]
        acc = m.sbuf("acc", [128, 2, SC])
        prod = m.sbuf("prod", [128, SUBS, len(POOL_TAPS), SC])
        deep = m.sbuf("deep", [128, JOBS_PAIR, ROWS * S])
        out = m.sbuf("out", [C, 2, ROWS, S])
        ps_e = m.psum("ps_e", [128, 2, BANK])
        ps_t = m.psum("ps_t", [128, 2, 2, BANK])
        ps_o = m.psum("ps_o", [C, 2, BANK])

        w_in = m.sem("w_in")
        passed = m.sem("passed")
        x_in = [m.sem(f"x_in{i}") for i in range(2)]
        out_out = [m.sem(f"out_out{i}") for i in range(2)]
        cleared = m.sem("cleared")
        bn_log = m.sem("bn_log")
        bn_rs = m.sem("bn_rs")
        bn_scale = m.sem("bn_scale")
        bn_shift = m.sem("bn_shift")
        w3_ready = m.sem("w3_ready")
        prep_done = m.sem("prep_done")
        exp_ready = m.sem("exp_ready")
        hid_done = m.sem("hid_done")
        taps_ready = m.sem("taps_ready")
        dve_tap = m.sem("dve_tap")
        dve_done = m.sem("dve_done")
        prod_ready = m.sem("prod_ready")
        pool_mid = m.sem("pool_mid")
        pool_done = m.sem("pool_done")
        deep_done = m.sem("deep_done")
        proj_ready = m.sem("proj_ready")
        out_done = m.sem("out_done")

        def job(i):
            img, rest = divmod(i, JOBS_IMG)
            pair, k = divmod(rest, JOBS_PAIR)
            return img, pair, k, (k if k < 4 else 4 if k == 4 else k - 5)

        def strips_of(pair, k):
            if k < 4:
                return [(pair, 0, 128)]
            if k == 4:
                return [(pair, 0, 64), (pair + PAIRS, 64, 64)]
            return [(pair + PAIRS, 0, 128)]

        def runs(first, n):
            found = []
            for r in range(first, first + n):
                c = min(max(r, 0), S - 1)
                last = found[-1] if found else None
                if last and last[1] + last[2] == c and c != HQ and c == r and last[3]:
                    last[2] += 1
                else:
                    found.append([r - first, c, 1, c == r])
            return [(at, c, k) for at, c, k, _ in found]

        def pieces_after(i):
            img, pair, k, _ = job(i)
            if 5 <= k:
                return [(img, pair, 0, k - 5)]
            if k < 4:
                if pair > 0:
                    return [(img, pair - 1, 1, k)]
                if img == 1:
                    return [(0, PAIRS - 1, 1, k)]
            return []

        all_pieces = []
        after = []
        for i in range(JOBS):
            after.append(pieces_after(i))
            all_pieces += after[-1]
        drain = [(1, PAIRS - 1, 1, g) for g in range(PIECES)]
        all_pieces += drain
        NPIECE = len(all_pieces)
        number = {p: n for n, p in enumerate(all_pieces)}
        NSTRIP = NPIECE // PIECES

        edge_written = m.sem("edge_written")

        def edge_jobs():
            found = []
            for i in range(1, JOBS + 1):
                img, pair, k, t = job(i % JOBS)
                for rnd in range(2):
                    for strip, p0, np_ in strips_of(pair, k):
                        if (strip == 0 and rnd == 0) or (strip == 2 * PAIRS - 1 and rnd == 1):
                            found.append((i, rnd))
            return found

        edges = len(edge_jobs())

        def edge_count(i, rnd):
            if i == 0:
                return 1
            return 2 + edge_jobs().index((i, rnd))

        def pieces_before(i):
            img, pair, k, t = job(i)
            g = img * PAIRS + pair - 1
            if g < 0:
                return 0
            pimg, ppair = divmod(g, PAIRS)
            b = 0 if k < 4 else 1
            return number[(pimg, ppair, b, PIECES - 1)] + 1

        def ps_o_w(t):
            return ps_t[:, t // 4, 0, (t % 4) * C:(t % 4 + 1) * C]

        m.start()
        nc_block = ctx.enter_context(nc.Block())

        @nc_block.sync
        def _(sp):
            for tile, name in ((w1, "w1"), (w3, "w3"), (wd, "wd"), (bn, "bn"), (bn3, "bn3"), (ident, "ident")):
                sp.dma_start(tile[tuple([slice(None)] * len(tile.shape))], d[name]).then_inc(w_in, 16)

            def load(parity, image):
                sp.dma_start(x[parity][:, :, :, :].rearrange("c q h w -> c q (h w)"),
                             d["x1_img"][:, ds(image, 1), :, :].rearrange("q b c l -> c (b q) l")).then_inc(x_in[parity], 16)

            load(0, 0)
            with sp.Fori(0, imgs // 2) as it:
                after_next = sp.snap((it * 2 + 2) % imgs)
                sp_wait(sp, passed, (out_done, ONE + CREDIT + it * NPIECE))
                load(1, it * 2 + 1)
                done = 0
                for n, (img, pair, b, g) in enumerate(all_pieces):
                    if g < PIECES - 1:
                        continue
                    sp_wait(sp, passed, (out_done, ONE + CREDIT + it * NPIECE + (n + 1)))
                    strip = pair + b * PAIRS
                    par = (n // PIECES) % 2
                    sp.dma_start(d["out"][ds(it * 2 + img, 1), :, strip * ROWS:(strip + 1) * ROWS, :]
                                 .rearrange("a c h w -> (a c) h w"), out[:, par, :, :]).then_inc(out_out[par], 16)
                    if (img, pair, b) == (0, PAIRS - 1, 1):
                        load(0, after_next)
            for i in range(2):
                sp_wait(sp, passed, (out_out[i], ONE + 16 * (NSTRIP // 2) * (imgs // 2)))
            sp_wait(sp, passed, (x_in[0], ONE + 16 * (imgs // 2 + 1)))

        @nc_block.tensor
        def _(pe):
            def expand(it, i):
                img, pair, k, t = job(i % JOBS)
                nxt = i // JOBS
                pe.wait_ge(x_in[img], ONE + 16 * (it + nxt + 1))
                for rnd, (row, n) in enumerate(((0, 5), (10, 4))):
                    pe.wait_ge(hid_done, ONE + it * (2 * JOBS) + (2 * i + rnd))
                    for b in range(2):
                        for strip, p0, np_ in strips_of(pair, k):
                            for at, src, cnt in runs(strip * ROWS - 1 + row + b * n, n):
                                half, loc = divmod(src, HQ)
                                rhs = x[img][:, 2 * half:2 * half + 2, loc:loc + cnt, :].rearrange("c q r w -> c r q w")
                                dst = ps_e[p0:p0 + np_, b, at * S:(at + cnt) * S].rearrange("p (r q w) -> p r q w", q=2, w=HQ)
                                mm = pe.matmul(dst, w1[:, t * 128:t * 128 + np_], rhs, start=True, stop=True)
                    mm.then_inc(exp_ready, 1)

            def taps(it, i, sub):
                img, pair, k, t = job(i)
                u = it * (2 * JOBS) + (2 * i + sub)
                pe.wait_ge(hid_done, ONE + it * (2 * JOBS) + 2 * (i + 1))
                pe.wait_ge(dve_done, ONE + CREDIT + u - 1)
                for n, tap in enumerate(PE_TAPS):
                    dy, dx = TAPS[tap]
                    for b in range(2):
                        r = sub * SR + b * BR + dy
                        mm = pe.matmul(ps_t[:, sub, b, 0:BR * S].rearrange("p (r w) -> p r w", w=S), diag[:, t, n, :],
                                       hid[i % 2][:, r:r + BR, dx:dx + S], start=(n == 0), stop=(n == len(PE_TAPS) - 1))
                mm.then_inc(taps_ready, 1)

            def project(it, piece):
                img, pair, b, g = piece
                n = it * NPIECE + number[piece]
                last = (img * PAIRS + pair) * JOBS_PAIR + (4 if b == 0 else 8)
                pe.wait_ge(deep_done, ONE + CREDIT + it * (2 * JOBS) + 2 * (last + 1))
                pe.wait_ge(out_done, ONE + CREDIT + n - 1)
                cols = slice(g * BR * S, (g + 1) * BR * S)
                dst = ps_o[:, number[piece] % 2, 0:BR * S]
                for t in range(4):
                    pe.matmul(dst, w3s[:, t, :], deep[:, 5 * b + t, cols], start=(t == 0), stop=False)
                p0 = 64 * b
                pe.matmul(dst, w3s[p0:p0 + 64, 4, :], deep[p0:p0 + 64, 4, cols], start=False, stop=True).then_inc(proj_ready, 1)

            pe.wait_ge(bn_shift, ONE + 3)
            for t in range(5):
                n = 128 if t < 4 else 64
                for p0 in ([0] if t < 4 else [0, 64]):
                    bank, at = (0, t) if t < 4 else (1, 0)
                    mm = pe.matmul(ps_o_w(t)[p0:p0 + n, :], w3[:, t * 128:t * 128 + n], diag3[:, :], start=True, stop=True)
            mm.then_inc(w3_ready, 1)
            pe.wait_ge(prep_done, ONE + 1)
            expand(0, 0)
            with pe.Fori(0, imgs // 2) as it:
                for i in range(JOBS):
                    taps(it, i, 0)
                    expand(it, i + 1)
                    taps(it, i, 1)
                    for piece in after[i]:
                        project(it, piece)
                for piece in drain:
                    project(it, piece)

        @nc_block.scalar
        def _(act):
            def evac(it, i, rnd):
                img, pair, k, t = job(i % JOBS)
                e = it * (2 * JOBS) + (2 * i + rnd)
                row, n = ((0, 5), (10, 4))[rnd]
                act.wait_ge(exp_ready, ONE + e + 1)
                act.wait_ge(dve_done, ONE + CREDIT + it * (2 * JOBS) + 2 * (i - 1))
                if i > 0:
                    act.wait_ge(prod_ready, ONE + it * (2 * JOBS) + 2 * (i - 1))
                dst = hid[i % 2][:, row:row + 2 * n, 1:1 + S].rearrange("p (b r) w -> p b r w", b=2)
                src = ps_e[:, :, 0:n * S].rearrange("p b (r w) -> p b r w", w=S)
                ins = act.activation(dst, src, ACT.Relu, bias=bi[:, t, 0:1], scale=sc[:, t, 0:1])
                for strip, p0, np_ in strips_of(pair, k):
                    edge = 0 if strip == 0 and rnd == 0 else HT - 1 if strip == 2 * PAIRS - 1 and rnd == 1 else None
                    if edge is not None:
                        ins.then_inc(edge_written, 1)
                        act.wait_ge(edge_written, ONE + it * edges + edge_count(i, rnd))
                        ins = act.activation(hid[i % 2][p0:p0 + np_, edge, 1:1 + S], zeros[p0:p0 + np_, :], ACT.Copy)
                ins.then_inc(hid_done, 1)

            def products(it, i, sub):
                img, pair, k, t = job(i)
                u = it * (2 * JOBS) + (2 * i + sub)
                act.wait_ge(hid_done, ONE + it * (2 * JOBS) + 2 * (i + 1))
                act.wait_ge(pool_done, ONE + CREDIT + u - 1)
                for n, tap in enumerate(POOL_TAPS):
                    dy, dx = TAPS[tap]
                    r = sub * SR + dy
                    ins = act.activation(prod[:, sub, n, :].rearrange("p (r w) -> p r w", w=S), hid[i % 2][:, r:r + SR, dx:dx + S],
                                         ACT.Copy, scale=wd[:, t, tap:tap + 1])
                ins.then_inc(prod_ready, 1)

            def deepen(it, i, sub):
                img, pair, k, t = job(i)
                u = it * (2 * JOBS) + (2 * i + sub)
                act.wait_ge(pool_done, ONE + CREDIT + u + 1)
                if sub == 0:
                    n = pieces_before(i)
                    act.wait_ge(proj_ready, ONE + it * NPIECE + n)
                act.activation(deep[:, k, sub * SC:(sub + 1) * SC], acc[:, sub, :], ACT.Relu, bias=bi[:, t, 1:2],
                               scale=sc[:, t, 1:2]).then_inc(deep_done, 1)

            act.preload_act_table_set(LN_EXP)
            act.wait_ge(w_in, ONE + 16 * 6)
            act.wait_ge(cleared, ONE + 4)
            act.activation(sc[:, :, 0], bn[:, :, 3], ACT.Ln, bias=eps[:, 0:1])
            act.activation(sc[:, :, 1], bn[:, :, 7], ACT.Ln, bias=eps[:, 0:1])
            act.activation(sc3[:, :], bn3[:, 3:4], ACT.Ln, bias=eps[0:C, 0:1]).then_inc(bn_log, 1)
            act.wait_ge(bn_log, ONE + 1)
            act.activation(sc[:, :, :], sc[:, :, :], ACT.Exp, scale=-0.5)
            act.activation(sc3[:, :], sc3[:, :], ACT.Exp, scale=-0.5).then_inc(bn_rs, 1)
            act.wait_ge(bn_shift, ONE + 3)
            evac(0, 0, 0)
            evac(0, 0, 1)
            with act.Fori(0, imgs // 2) as it:
                for i in range(JOBS):
                    products(it, i, 0)
                    evac(it, i + 1, 0)
                    if i > 0:
                        deepen(it, i - 1, 1)
                    evac(it, i + 1, 1)
                    products(it, i, 1)
                    deepen(it, i, 0)
                deepen(it, JOBS - 1, 1)

        @nc_block.vector
        def _(dve):
            def depthwise(it, i, sub):
                img, pair, k, t = job(i)
                u = it * (2 * JOBS) + (2 * i + sub)
                dve.wait_ge(hid_done, ONE + it * (2 * JOBS) + 2 * (i + 1))
                dve.wait_ge(taps_ready, ONE + u + 1)
                psum = ps_t[:, sub, :, 0:BR * S].rearrange("p b (r w) -> p b r w", w=S)
                for n, tap in enumerate(DVE_TAPS):
                    dy, dx = TAPS[tap]
                    r = sub * SR + dy
                    src = hid[i % 2][:, r:r + SR, dx:dx + S].rearrange("p (b r) w -> p b r w", b=2)
                    last = n == len(DVE_TAPS) - 1
                    if n:
                        dve.wait_ge(dve_tap, ONE + u * (len(DVE_TAPS) - 1) + n)
                    if last:
                        dve.wait_ge(deep_done, ONE + CREDIT + u - 1)
                    dst = acc[:, sub, :].rearrange("p (b r w) -> p b r w", b=2, w=S) if last else psum
                    dve.scalar_tensor_tensor(out=dst, in0=src, scalar=wd[:, t, tap:tap + 1], in1=psum,
                                             op0=ALU.mult, op1=ALU.add).then_inc(dve_done if last else dve_tap, 1)

            def residual(it, piece):
                img, pair, b, g = piece
                num = number[piece]
                dve.wait_ge(proj_ready, ONE + it * NPIECE + num + 1)
                strip = num // PIECES
                if g == 0:
                    dve.wait_ge(out_out[strip % 2], ONE + 16 * (it * (NSTRIP // 2) + strip // 2))
                row = (pair + b * PAIRS) * ROWS + g * BR
                half, loc = divmod(row, HQ)
                for q in range(2):
                    src = ps_o[:, num % 2, 0:BR * S].rearrange("p (r q w) -> p r q w", q=2, w=HQ)[:, :, q, :]
                    ins = dve.scalar_tensor_tensor(out=out[:, strip % 2, g * BR:(g + 1) * BR, q * HQ:(q + 1) * HQ], in0=src,
                                                   scalar=bi3[:, 0:1], in1=x[img][:, 2 * half + q, loc:loc + BR, :],
                                                   op0=ALU.add, op1=ALU.add)
                ins.then_inc(out_done, 1)

            for i in range(2):
                dve.memset(hid[i][:, :, :], 0.0).then_inc(cleared, 1)
            dve.memset(zeros[:, :], 0.0).then_inc(cleared, 1)
            dve.memset(eps[:, :], BN_EPS).then_inc(cleared, 1)
            dve.memset(acc[:, 0, 0:1], 0.0).then_inc(dve_done, CREDIT)
            dve.memset(acc[:, 0, 1:2], 0.0).then_inc(out_done, CREDIT)
            dve.memset(acc[:, 0, 3:4], 0.0).then_inc(deep_done, CREDIT)
            dve.wait_ge(w_in, ONE + 16 * 6)
            dve.wait_ge(bn_rs, ONE + 1)
            dve.tensor_tensor(sc[:, :, 0], sc[:, :, 0], bn[:, :, 0], ALU.mult)
            dve.tensor_tensor(sc[:, :, 1], sc[:, :, 1], bn[:, :, 4], ALU.mult)
            dve.tensor_tensor(sc3[:, :], sc3[:, :], bn3[:, 0:1], ALU.mult).then_inc(bn_scale, 1)
            dve.wait_ge(bn_scale, ONE + 1)
            dve.tensor_tensor(bi[:, :, 0], sc[:, :, 0], bn[:, :, 2], ALU.mult)
            dve.tensor_tensor(bi[:, :, 1], sc[:, :, 1], bn[:, :, 6], ALU.mult)
            dve.tensor_tensor(bi3[:, :], sc3[:, :], bn3[:, 2:3], ALU.mult)
            dve.tensor_scalar(diag3[:, :], ident[0:C, 0:C], sc3[:, 0:1], None, ALU.mult)
            for t in range(5):
                for n, tap in enumerate(PE_TAPS):
                    dve.tensor_scalar(diag[:, t, n, :], ident[:, :], wd[:, t, tap:tap + 1], None, ALU.mult)
            dve.memset(acc[:, 0, 2:3], 0.0).then_inc(bn_scale, 1)
            dve.wait_ge(bn_scale, ONE + 2)
            dve.tensor_tensor(bi[:, :, 0], bn[:, :, 1], bi[:, :, 0], ALU.subtract).then_inc(bn_shift, 1)
            dve.tensor_tensor(bi[:, :, 1], bn[:, :, 5], bi[:, :, 1], ALU.subtract).then_inc(bn_shift, 1)
            dve.tensor_tensor(bi3[:, :], bn3[:, 1:2], bi3[:, :], ALU.subtract).then_inc(bn_shift, 1)
            dve.wait_ge(w3_ready, ONE + 1)
            for t in range(5):
                ins = dve.tensor_copy(w3s[:, t, :], ps_o_w(t))
            ins.then_inc(prep_done, 1)
            with dve.Fori(0, imgs // 2) as it:
                for i in range(JOBS):
                    for sub in range(2):
                        depthwise(it, i, sub)
                    if i > 0:
                        for piece in after[i - 1]:
                            residual(it, piece)
                for piece in after[JOBS - 1] + drain:
                    residual(it, piece)

        @nc_block.gpsimd
        def _(pool):
            pool.memset(prod[:, 0, 0, 0:1], 0.0).then_inc(pool_done, CREDIT)
            with pool.Fori(0, imgs // 2) as it:
                for i in range(JOBS):
                    for sub in range(2):
                        u = it * (2 * JOBS) + (2 * i + sub)
                        pool.wait_ge(prod_ready, ONE + u + 1)
                        for n in range(1, len(POOL_TAPS)):
                            pool.tensor_tensor(prod[:, sub, 0, :], prod[:, sub, 0, :], prod[:, sub, n, :], ALU.add).then_inc(pool_mid, 1)
                            pool.wait_ge(pool_mid, ONE + u * (len(POOL_TAPS) - 1) + n)
                        pool.wait_ge(dve_done, ONE + CREDIT + u + 1)
                        pool.tensor_tensor(acc[:, sub, :], acc[:, sub, :], prod[:, sub, 0, :], ALU.add).then_inc(pool_done, 1)


def build(nc, d):
    imgs = d["x"].shape[1]
    total = NQ * imgs
    sets = total // IMGS

    def scratch(name, shape, dtype=F32):
        return nc.dram_tensor(f"scratch_{name}", shape, dtype, kind="Internal").ap()

    d["x_flat"] = d["x"].rearrange("q b c l -> (q b c) l")
    d["z"] = scratch("z", (2, total * C, L))
    d["y"] = scratch("y", (2, total * C, L))
    d["a"] = scratch("a", (total * C, L))
    d["bc"] = scratch("bc", (sets, 2, 2, 2, IMGS, PARTS * N, L), BF16)
    d["dts4"] = scratch("dts", (sets, 2, 2, IMGS, R, L))
    d["dts"] = d["dts4"].rearrange("s o r i k l -> s o r (i k) l")
    x1 = scratch("x1", (NQ, imgs, C, L))
    d["x1"] = x1.rearrange("q b c l -> (q b c) l")
    d["x1_img"] = x1
    front_phase(nc, d)
    scan_phase(nc, d)
    gate_phase(nc, d)
    residual_phase(nc, d)


def layouts(i):
    f = np.float32
    a = {}
    imgs = i["x"].shape[0]
    tiles = NQ * imgs * C // 128
    a["x"] = i["x"].reshape(imgs, C, 2, HQ, 2, HQ).transpose(2, 4, 0, 1, 3, 5).reshape(NQ, imgs, C, L)
    lead = lambda w: w.transpose(2, 0, 1)
    a["p1_w"] = lead(i["L0_conv_p1_w"])
    a["p2in_w"] = lead(i["L0_conv_p2in_w"])
    a["dw_w"] = i["L0_conv_dw_w"].reshape(NQ, C, 9).transpose(1, 0, 2)
    a["front_vec"] = np.stack([i["L0_conv_" + n].T for n in ("ln_g", "ln_b", "p1_b", "p2in_b", "dw_b")], axis=2)
    a["gate_vec"] = np.stack([i["L0_conv_" + n].T for n in ("ssln_g", "ssln_b", "p2n_g", "p2n_b", "ca_b2")], axis=2)
    a["ca_w1"] = lead(i["L0_conv_ca_w1"])
    a["ca_w2"] = lead(i["L0_conv_ca_w2"])
    a["ca_b1"] = i["L0_conv_ca_b1"].T
    xw = i["L0_conv_xproj_w"]
    wx = np.zeros((C, NQ, 2, 64), f)
    prm = np.zeros((NQ, 2, C, 2 * N + 4), f)
    for o in range(2):
        for r in range(2):
            k = o + 2 * r
            wx[:, :, o, 8 * r:8 * r + N] = xw[:, k, R:R + N].transpose(2, 0, 1)
            wx[:, :, o, 16 + 8 * r:16 + 8 * r + N] = xw[:, k, R + N:R + 2 * N].transpose(2, 0, 1)
            wx[:, :, o, 32 + R * r:32 + R * (r + 1)] = xw[:, k, 0:R].transpose(2, 0, 1)
            prm[:, o, :, r * N:(r + 1) * N] = i["L0_conv_A_logs"][:, k]
            prm[:, o, :, 2 * N + r] = i["L0_conv_Ds"][:, k]
            prm[:, o, :, 2 * N + 2 + r] = i["L0_conv_dtproj_b"][:, k]
    a["xproj_w"] = wx
    packed = np.repeat(prm[:, None], imgs, axis=1).transpose(2, 0, 1, 3, 4).reshape(2, tiles, 128, 2 * N + 4)
    a["prm"] = packed.transpose(1, 0, 2, 3)
    wdt = np.zeros((tiles, 2, IMGS * R, 2, 128), f)
    select = np.zeros((TILES, IMGS * PARTS * N, N, 128), f)
    per_q = tiles // NQ
    for t in range(TILES):
        for p in range(128):
            img, c = divmod(t * 128 + p, C)
            for n in range(N):
                select[t, [img * PARTS * N + j * N + n for j in range(PARTS)], n, p] = 1.0
            for o in range(2):
                for r in range(2):
                    for q in range(NQ):
                        wdt[q * per_q + t:(q + 1) * per_q:TILES, o, img * R:(img + 1) * R, r, p] = i["L0_conv_dtproj_w"][q, o + 2 * r, c]
    a["wdt"] = wdt
    a["select"] = select.astype(mybir.dt.np(BF16))
    a["ident"] = np.eye(128, dtype=f)
    a["mean"] = np.full((C, C), 1.0 / C, f)
    a["center"] = np.eye(C, dtype=f) - np.full((C, C), 1.0 / C, f)
    hidden = np.concatenate([np.arange(576), np.arange(512, 576)])
    a["w1"] = i["L1_conv_w1"].reshape(576, C).T
    a["w3"] = i["L1_conv_w3"].reshape(C, 576)
    a["wd"] = i["L1_conv_wd"].reshape(576, 9)[hidden].reshape(5, 128, 9).transpose(1, 0, 2)
    bn = np.stack([i["L1_conv_" + n] for n in ("g1", "b1", "m1", "v1", "g2", "b2", "m2", "v2")], axis=1)
    a["bn"] = bn[hidden].reshape(5, 128, 8).transpose(1, 0, 2)
    a["bn3"] = np.stack([i["L1_conv_" + n] for n in ("g3", "b3", "m3", "v3")], axis=1)
    return {k: np.ascontiguousarray(v) for k, v in a.items()}


def kernel(**inputs):
    import concourse.bacc as bacc
    from concourse.bass_utils import run_bass_kernel_spmd

    nc = bacc.Bacc("TRN2", target_bir_lowering=False, num_devices=1)
    inputs = {k: np.asarray(v) for k, v in inputs.items()}
    arrays = {f"in_{k}_dram": v for k, v in layouts(inputs).items()}
    d = {}
    for name, v in arrays.items():
        d[name[3:-5]] = nc.dram_tensor(name, v.shape, mybir.dt.from_np(v.dtype), kind="ExternalInput").ap()
    d["out"] = nc.dram_tensor("out_0_dram", inputs["x"].shape, F32, kind="ExternalOutput").ap()
    build(nc, d)
    r = run_bass_kernel_spmd(nc, [arrays], core_ids=[0])
    return r.results[0]["out_0_dram"]
```
